# Optimizing a Trainium2 kernel written in Bass

```python
import numpy as np
import jax
import jax.numpy as jnp

def _softmax(x, axis=-1):
    return jax.nn.softmax(x, axis=axis)

def _gelu(x):
    return jax.nn.gelu(x, approximate=True)

def _silu(x):
    return jax.nn.silu(x)

def _sigmoid(x):
    return jax.nn.sigmoid(x)

def _layernorm(x, axis=-1, eps=1e-05):
    m = jnp.mean(x, axis=axis, keepdims=True)
    v = jnp.var(x, axis=axis, keepdims=True)
    return (x - m) / jnp.sqrt(v + eps)

def _scatter_add(tgt, idx, src, axis=0):
    return tgt.at[idx].add(src)

def _segment_sum(src, seg, n):
    return jax.ops.segment_sum(src, seg, n)
kernel_name = 'mk_gnn_preln_d4_gnn_r8_b04897'

def setup_inputs(seed: int=0):
    np.random.seed(seed)
    _w = jnp.asarray

    def _rec_inputs():
        import jax
        import jax.numpy as jnp
        _gk = jax.random.key(seed)
        x = -0.0001006 + 1 * jax.random.normal(jax.random.fold_in(_gk, 1), (6250, 96), jnp.float32)
        src = jax.random.randint(jax.random.fold_in(_gk, 2), (200000,), 0, 6250, jnp.int32)
        dst = jnp.minimum((6250 * jax.random.uniform(jax.random.fold_in(_gk, 3), (200000,)) ** 2.0).astype(jnp.int32), 49999)
        _o = jnp.argsort(dst, stable=True)
        src = src[_o]
        dst = dst[_o]
        edge_attr_17 = jax.random.uniform(jax.random.fold_in(_gk, 11), (200000, 17), jnp.float32, 0.0, 1)
        edge_attr_32 = 0.000196303 + 1.00016 * jax.random.normal(jax.random.fold_in(_gk, 12), (200000, 32), jnp.float32)
        return (x, src, dst, edge_attr_17, edge_attr_32)
    x, src, dst, edge_attr_17, edge_attr_32 = _rec_inputs()

    def _L0_gnn_setup():
        import jax, jax.numpy as jnp
        import numpy as np
        N_NODES = 6250
        N_EDGES = 100000
        D_IN = 96
        D_OUT = 96
        key = jax.random.key(seed)
        k1, k2, k3, k4 = jax.random.split(key, 4)
        x = jax.random.normal(k1, (N_NODES, D_IN), dtype=jnp.float32)
        edge_index = jax.random.randint(k2, (2, N_EDGES), 0, N_NODES, dtype=jnp.int64)
        W = jax.random.normal(k3, (D_IN, D_OUT), dtype=jnp.float32) * (1.0 / np.sqrt(D_IN))
        b = jax.random.normal(k4, (D_OUT,), dtype=jnp.float32) * 0.01
        return {'x': x, 'edge_index': edge_index, 'W': W, 'b': b}
    _L0_gnn_all = _L0_gnn_setup()
    _L0_gnn_in = {k: v for k, v in _L0_gnn_all.items() if k in ('W', 'b')}
    del _L0_gnn_all

    def _L1_gnn_setup():
        import jax, jax.numpy as jnp
        import numpy as np
        N, E = (6250, 100000)
        ND, ED = (96, 32)

        def _gelu(x):
            return jax.nn.gelu(x, approximate=False)
        key = jax.random.key(seed)
        ks = jax.random.split(key, 16)
        s = lambda fan_in: 1.0 / np.sqrt(fan_in)
        inp = {'x': jax.random.normal(ks[0], (N, ND), jnp.float32), 'edge_index': jax.random.randint(ks[1], (2, E), 0, N, jnp.int32), 'edge_attr': jax.random.normal(ks[2], (E, ED), jnp.float32), 'mW1': jax.random.uniform(ks[3], (ND + ED, ND), jnp.float32, -s(ND + ED), s(ND + ED)), 'mb1': jnp.zeros((ND,), jnp.float32), 'mW2': jax.random.uniform(ks[4], (ND, ND), jnp.float32, -s(ND), s(ND)), 'mb2': jnp.zeros((ND,), jnp.float32), 'gW1': jax.random.uniform(ks[5], (ND + ED, ND), jnp.float32, -s(ND + ED), s(ND + ED)), 'gb1': jnp.zeros((ND,), jnp.float32), 'gW2': jax.random.uniform(ks[6], (ND, 1), jnp.float32, -s(ND), s(ND)), 'gb2': jnp.zeros((1,), jnp.float32), 'uW1': jax.random.uniform(ks[7], (2 * ND, ND), jnp.float32, -s(2 * ND), s(2 * ND)), 'ub1': jnp.zeros((ND,), jnp.float32), 'uW2': jax.random.uniform(ks[8], (ND, ND), jnp.float32, -s(ND), s(ND)), 'ub2': jnp.zeros((ND,), jnp.float32), 'ln_g': jnp.ones((ND,), jnp.float32), 'ln_b': jnp.zeros((ND,), jnp.float32)}
        return inp
    _L1_gnn_all = _L1_gnn_setup()
    _L1_gnn_in = {k: v for k, v in _L1_gnn_all.items() if k in ('mW1', 'mb1', 'mW2', 'mb2', 'gW1', 'gb1', 'gW2', 'gb2', 'uW1', 'ub1', 'uW2', 'ub2', 'ln_g', 'ln_b')}
    del _L1_gnn_all

    def _L2_gnn_setup():
        import jax, jax.numpy as jnp
        import numpy as np
        N = 6250
        E = 100000
        D = 96
        ED = 17
        key = jax.random.key(seed)
        ks = jax.random.split(key, 12)
        x = jax.random.normal(ks[0], (N, D), dtype=jnp.float32)
        edge_index = jax.random.randint(ks[1], (2, E), 0, N, dtype=jnp.int64)
        edge_attr = jax.random.uniform(ks[2], (E, ED), dtype=jnp.float32)
        s = 1.0 / np.sqrt(ED)
        W1 = jax.random.uniform(ks[3], (D, ED), jnp.float32, -s, s)
        b1 = jax.random.uniform(ks[4], (D,), jnp.float32, -s, s)
        s = 1.0 / np.sqrt(D)
        W2 = jax.random.uniform(ks[5], (D, D), jnp.float32, -s, s)
        b2 = jax.random.uniform(ks[6], (D,), jnp.float32, -s, s)
        Ws = jax.random.uniform(ks[7], (D, D), jnp.float32, -s, s)
        bs = jax.random.uniform(ks[8], (D,), jnp.float32, -s, s)
        Wn = jax.random.uniform(ks[9], (D, D), jnp.float32, -s, s)
        bn = jax.random.uniform(ks[10], (D,), jnp.float32, -s, s)
        return {'x': x, 'edge_index': edge_index, 'edge_attr': edge_attr, 'W1': W1, 'b1': b1, 'W2': W2, 'b2': b2, 'Ws': Ws, 'bs': bs, 'Wn': Wn, 'bn': bn}
    _L2_gnn_all = _L2_gnn_setup()
    _L2_gnn_in = {k: v for k, v in _L2_gnn_all.items() if k in ('W1', 'b1', 'W2', 'b2', 'Ws', 'bs', 'Wn', 'bn')}
    del _L2_gnn_all

    def _L3_gnn_setup():
        import jax, jax.numpy as jnp
        import numpy as np
        N_NODES = 6250
        N_EDGES = 100000
        D = 96
        N_LAYERS = 3
        key = jax.random.key(seed)
        ks = jax.random.split(key, 8)
        s = 1.0 / np.sqrt(D)
        x = jax.random.normal(ks[0], (N_NODES, D), dtype=jnp.float32)
        edge_index = jax.random.randint(ks[1], (2, N_EDGES), 0, N_NODES, dtype=jnp.int32)
        W_in = jax.random.normal(ks[2], (D, D), dtype=jnp.float32) * s
        b_in = jnp.zeros((D,), dtype=jnp.float32)
        gcn_W = jax.random.normal(ks[3], (N_LAYERS, D, D), dtype=jnp.float32) * s
        gcn_b = jnp.zeros((N_LAYERS, D), dtype=jnp.float32)
        W_out = jax.random.normal(ks[4], (D, D), dtype=jnp.float32) * s
        b_out = jnp.zeros((D,), dtype=jnp.float32)
        return {'x': x, 'edge_index': edge_index, 'W_in': W_in, 'b_in': b_in, 'gcn_W': gcn_W, 'gcn_b': gcn_b, 'W_out': W_out, 'b_out': b_out}
    _L3_gnn_all = _L3_gnn_setup()
    _L3_gnn_in = {k: v for k, v in _L3_gnn_all.items() if k in ('W_in', 'b_in', 'gcn_W', 'gcn_b', 'W_out', 'b_out')}
    del _L3_gnn_all
    return {'x': x, 'src': src, 'dst': dst, 'edge_attr_17': edge_attr_17, 'edge_attr_32': edge_attr_32, 'L0_gnn_W': _L0_gnn_in['W'], 'L0_gnn_b': _L0_gnn_in['b'], 'L1_gnn_mW1': _L1_gnn_in['mW1'], 'L1_gnn_mb1': _L1_gnn_in['mb1'], 'L1_gnn_mW2': _L1_gnn_in['mW2'], 'L1_gnn_mb2': _L1_gnn_in['mb2'], 'L1_gnn_gW1': _L1_gnn_in['gW1'], 'L1_gnn_gb1': _L1_gnn_in['gb1'], 'L1_gnn_gW2': _L1_gnn_in['gW2'], 'L1_gnn_gb2': _L1_gnn_in['gb2'], 'L1_gnn_uW1': _L1_gnn_in['uW1'], 'L1_gnn_ub1': _L1_gnn_in['ub1'], 'L1_gnn_uW2': _L1_gnn_in['uW2'], 'L1_gnn_ub2': _L1_gnn_in['ub2'], 'L1_gnn_ln_g': _L1_gnn_in['ln_g'], 'L1_gnn_ln_b': _L1_gnn_in['ln_b'], 'L2_gnn_W1': _L2_gnn_in['W1'], 'L2_gnn_b1': _L2_gnn_in['b1'], 'L2_gnn_W2': _L2_gnn_in['W2'], 'L2_gnn_b2': _L2_gnn_in['b2'], 'L2_gnn_Ws': _L2_gnn_in['Ws'], 'L2_gnn_bs': _L2_gnn_in['bs'], 'L2_gnn_Wn': _L2_gnn_in['Wn'], 'L2_gnn_bn': _L2_gnn_in['bn'], 'L3_gnn_W_in': _L3_gnn_in['W_in'], 'L3_gnn_b_in': _L3_gnn_in['b_in'], 'L3_gnn_gcn_W': _L3_gnn_in['gcn_W'], 'L3_gnn_gcn_b': _L3_gnn_in['gcn_b'], 'L3_gnn_W_out': _L3_gnn_in['W_out'], 'L3_gnn_b_out': _L3_gnn_in['b_out']}

def reference(x, src, dst, edge_attr_17, edge_attr_32, L0_gnn_W, L0_gnn_b, L1_gnn_mW1, L1_gnn_mb1, L1_gnn_mW2, L1_gnn_mb2, L1_gnn_gW1, L1_gnn_gb1, L1_gnn_gW2, L1_gnn_gb2, L1_gnn_uW1, L1_gnn_ub1, L1_gnn_uW2, L1_gnn_ub2, L1_gnn_ln_g, L1_gnn_ln_b, L2_gnn_W1, L2_gnn_b1, L2_gnn_W2, L2_gnn_b2, L2_gnn_Ws, L2_gnn_bs, L2_gnn_Wn, L2_gnn_bn, L3_gnn_W_in, L3_gnn_b_in, L3_gnn_gcn_W, L3_gnn_gcn_b, L3_gnn_W_out, L3_gnn_b_out):
    import jax
    import jax.numpy as jnp

    def _L0_gnn_ref(x, edge_index, W, b):
        import jax, jax.numpy as jnp
        import numpy as np
        N_NODES = 6250
        N_EDGES = 100000
        D_IN = 96
        D_OUT = 96
        num_nodes = x.shape[0]
        src, dst = (edge_index[0], edge_index[1])
        messages = x[src] @ W + b
        out = jax.ops.segment_sum(messages, dst, num_segments=num_nodes)
        deg = jax.ops.segment_sum(jnp.ones((dst.shape[0],), dtype=x.dtype), dst, num_segments=num_nodes)
        deg = jnp.clip(deg, 1.0, None)
        return out / deg[:, None]

    def _L1_gnn_ref(x, edge_index, edge_attr, mW1, mb1, mW2, mb2, gW1, gb1, gW2, gb2, uW1, ub1, uW2, ub2, ln_g, ln_b):
        import jax, jax.numpy as jnp
        import numpy as np
        N, E = (6250, 100000)
        ND, ED = (96, 32)

        def _gelu(x):
            return jax.nn.gelu(x, approximate=False)
        src, dst = (edge_index[0], edge_index[1])
        edge_input = jnp.concatenate([x[src], edge_attr], axis=-1)
        messages = _gelu(edge_input @ mW1 + mb1) @ mW2 + mb2
        gates = jax.nn.sigmoid(_gelu(edge_input @ gW1 + gb1) @ gW2 + gb2)
        aggregated = jax.ops.segment_sum(messages * gates, dst, num_segments=x.shape[0])
        combined = jnp.concatenate([x, aggregated], axis=-1)
        update = _gelu(combined @ uW1 + ub1) @ uW2 + ub2
        h = x + update
        mu = jnp.mean(h, axis=-1, keepdims=True)
        var = jnp.mean(jnp.square(h - mu), axis=-1, keepdims=True)
        return (h - mu) * jax.lax.rsqrt(var + 1e-05) * ln_g + ln_b

    def _L2_gnn_ref(x, edge_index, edge_attr, W1, b1, W2, b2, Ws, bs, Wn, bn):
        import jax, jax.numpy as jnp
        import numpy as np
        N = 6250
        E = 100000
        D = 96
        ED = 17
        src, dst = (edge_index[0], edge_index[1])
        h = jax.nn.relu(edge_attr @ W1.T + b1)
        w = h @ W2.T + b2
        msg = w * x[src]
        agg = jax.ops.segment_sum(msg, dst, num_segments=x.shape[0])
        return jax.nn.relu(x @ Ws.T + bs + agg @ Wn.T + bn)

    def _L3_gnn_ref(x, edge_index, W_in, b_in, gcn_W, gcn_b, W_out, b_out):
        import jax, jax.numpy as jnp
        import numpy as np
        N_NODES = 6250
        N_EDGES = 100000
        D = 96
        N_LAYERS = 3
        N = x.shape[0]
        loop = jnp.arange(N, dtype=edge_index.dtype)
        row = jnp.concatenate([edge_index[0], loop])
        col = jnp.concatenate([edge_index[1], loop])
        deg = jax.ops.segment_sum(jnp.ones_like(col, dtype=x.dtype), col, num_segments=N)
        dinv = jnp.where(deg > 0, jax.lax.rsqrt(deg), 0.0)
        norm = (dinv[row] * dinv[col])[:, None]

        def gcn_conv(h, W, b):
            hw = h @ W.T
            msg = norm * hw[row]
            out = jax.ops.segment_sum(msg, col, num_segments=N)
            return out + b
        h = jax.nn.relu(x @ W_in.T + b_in)
        for l in range(N_LAYERS):
            h = h + jax.nn.relu(gcn_conv(h, gcn_W[l], gcn_b[l]))
        return h @ W_out.T + b_out
    edge_index = jnp.stack([src, dst])
    h = jnp.maximum(_layernorm(x, axis=-1), 0.0)
    x = x + _L0_gnn_ref(h, edge_index, L0_gnn_W, L0_gnn_b)
    h = jnp.maximum(_layernorm(x, axis=-1), 0.0)
    x = x + _L1_gnn_ref(h, edge_index, edge_attr_32, L1_gnn_mW1, L1_gnn_mb1, L1_gnn_mW2, L1_gnn_mb2, L1_gnn_gW1, L1_gnn_gb1, L1_gnn_gW2, L1_gnn_gb2, L1_gnn_uW1, L1_gnn_ub1, L1_gnn_uW2, L1_gnn_ub2, L1_gnn_ln_g, L1_gnn_ln_b)
    h = jnp.maximum(_layernorm(x, axis=-1), 0.0)
    x = x + _L2_gnn_ref(h, edge_index, edge_attr_17, L2_gnn_W1, L2_gnn_b1, L2_gnn_W2, L2_gnn_b2, L2_gnn_Ws, L2_gnn_bs, L2_gnn_Wn, L2_gnn_bn)
    h = jnp.maximum(_layernorm(x, axis=-1), 0.0)
    x = x + _L3_gnn_ref(h, edge_index, L3_gnn_W_in, L3_gnn_b_in, L3_gnn_gcn_W, L3_gnn_gcn_b, L3_gnn_W_out, L3_gnn_b_out)
    return x

_drawn_inputs = setup_inputs


def setup_inputs(seed=0):
    import zlib

    import numpy as np

    out = dict(_drawn_inputs(seed))
    spreads = {'L1_gnn_mb1': (0.0, 0.268),
     'L1_gnn_mb2': (0.0, 0.1),
     'L1_gnn_gb1': (0.0, 2.0),
     'L1_gnn_ub1': (0.0, 0.312),
     'L1_gnn_ub2': (0.0, 0.1),
     'L1_gnn_ln_g': (1.0, 0.2),
     'L1_gnn_ln_b': (0.0, 0.1),
     'L3_gnn_b_in': (0.0, 0.1),
     'L3_gnn_gcn_b': (0.0, 0.1),
     'L3_gnn_b_out': (0.0, 0.1)}
    factors = {'edge_attr_32': 2.904,
     'L0_gnn_b': 6.821,
     'L1_gnn_gW1': 8.0,
     'L1_gnn_gW2': 8.0,
     'L2_gnn_bs': 3.592,
     'L2_gnn_bn': 3.707}
    for name, (base, spread) in spreads.items():
        noise = np.random.default_rng([zlib.crc32(name.encode()), seed]).standard_normal(out[name].shape)
        drawn = base * np.exp(spread * noise) if base else spread * noise
        out[name] = jnp.asarray(drawn.astype(out[name].dtype))
    for name, factor in factors.items():
        out[name] = (out[name] * factor).astype(out[name].dtype)
    return out
```

```python
import numpy as np
import concourse.bass as bass
from concourse import mybir
from contextlib import ExitStack

F32 = mybir.dt.float32
I32 = mybir.dt.int32
ALU = mybir.AluOpType
ACT = mybir.ActivationFunctionType
AX = mybir.AxisListType
SP, PE, DVE, POOL, ACTE = (mybir.EngineType.SP, mybir.EngineType.PE, mybir.EngineType.DVE,
                           mybir.EngineType.Pool, mybir.EngineType.Activation)

P = 128
N, D, E = 6250, 96, 200000
EA, EB = 32, 17
NB = -(-N // P)
NP = NB * P
FULL = N // P
REST = N - FULL * P

SC = 16
COLS = -(-(-(-E // P)) // SC) * SC
LAST = E - (P - 1) * COLS
assert 0 < LAST <= COLS and LAST % SC == 0

G = 4
GPI = 6
TILES = (COLS * P + NB * (P - 1)) // P
TURNS = -(-TILES // (G * GPI))
Q = TURNS * GPI
T = Q * G
SLOTS = T * P

R_A, R_ONE_A, R_B, R_ONE_B = 0, EA, EA + 1, EA + 1 + EB
R_SRC, R_LANE = R_ONE_B + 1, R_ONE_B + 2
RW = R_LANE + 1
KA, KB = EA + 1, EB + 1

GB = 7
GS = NB // GB
EPS = 1e-5


class Signal:

    def __init__(self, ctx, nc, name):
        self.sem = ctx.enter_context(nc.semaphore(name))
        self.n = 0


def chain(eng, sig, ins):
    ins.then_inc(sig.sem, 1)
    sig.n += 1
    eng.wait_ge(sig.sem, sig.n)


def turns(eng, stages):
    def place(i, s, lag):
        q = i * GPI + (s - lag)
        if isinstance(i, int) and not 0 <= q < Q:
            return None
        return q, i if s >= lag else i - 1, (s - lag) % GPI

    def turn(i):
        for s in range(GPI):
            for work, *lags in stages:
                places = [place(i, s, lag) for lag in lags]
                if len(places) > 1 and any(places):
                    work(*places)
                elif places[0]:
                    work(*places[0])
    turn(0)
    with eng.Fori(1, TURNS) as i:
        turn(i)
    turn(TURNS)


def wait_past(eng, sem, base, q):
    if isinstance(q, int) and q <= 0:
        return
    eng.wait_ge(sem, base + q)


def graph_kernel(nc, x_in, src_in, dst_in, e17, e32, w):
    out_h = w["out"]
    top = ExitStack()
    with top:
        def sem(name):
            return Signal(top, nc, name)

        def sbuf(name, shape, dt=F32, ctx=top):
            return ctx.enter_context(nc.sbuf_tensor(name, shape, dt))

        rec_h = nc.dram_tensor("edge_records", (SLOTS, RW), F32, kind="Internal").ap()
        tab_h = nc.dram_tensor("node_rows", (NP, D), F32, kind="Internal").ap()
        tab2_h = nc.dram_tensor("node_rows_wide", (NP, 2 * D), F32, kind="Internal").ap()
        rec_groups = rec_h.rearrange("(q p j) w -> q p (j w)", p=P, j=G)
        tab_v = tab_h.rearrange("(b p) d -> p b d", p=P)
        tab2_v = tab2_h.rearrange("(b p) d -> p b d", p=P)

        x = sbuf("x", [P, NB, D])
        h = sbuf("h", [P, NB, D])
        accT = sbuf("accT", [D + 1, NP])
        src_all = sbuf("src_all", [P, T], I32)
        lane_all = sbuf("lane_all", [P, T])
        tile_col = sbuf("tile_col", [1, T], I32)
        rdeg = sbuf("rdeg", [P, NB])
        dinv = sbuf("dinv", [P, NB])
        iota = sbuf("iota", [P, P])
        ident = sbuf("ident", [P, P])
        s_sum = sbuf("s_sum", [P, NB])
        s_var = sbuf("s_var", [P, NB])
        s_std = sbuf("s_std", [P, NB])
        s_rstd = sbuf("s_rstd", [P, NB])

        w0 = sbuf("w0", [D + 1, D + 1])
        w1n = sbuf("w1n", [D, 2 * D])
        w1e = sbuf("w1e", [KA, 2 * D])
        w2m = sbuf("w2m", [D + 1, D])
        gw2 = sbuf("gw2", [P, D])
        gb2 = sbuf("gb2", [P, 1])
        half_gb2 = sbuf("half_gb2", [P, 1])
        u1x = sbuf("u1x", [D, D])
        u1a = sbuf("u1a", [D, D])
        ub1 = sbuf("ub1", [D, 1])
        u2 = sbuf("u2", [D + 1, D])
        lng = sbuf("lng", [P, D])
        lnb = sbuf("lnb", [P, D])
        w17 = sbuf("w17", [KB, D])
        w2w = sbuf("w2w", [D + 1, D])
        wsT = sbuf("wsT", [D + 1, D])
        bn_row = sbuf("bn_row", [D + 1, D])
        wnT = sbuf("wnT", [D, D])
        winT = sbuf("winT", [D + 1, D])
        gcnT = sbuf("gcnT", [D, 3, D])
        gcnb = sbuf("gcnb", [P, 3, D])
        woutT = sbuf("woutT", [D + 1, D])

        loaded = sem("loaded")
        made = sem("made")
        vec = sem("vec")
        act = sem("act")
        counted = sem("counted")
        offsets = sem("offsets")
        steps_up = sem("steps_up")
        columns = sem("columns")
        filled = sem("filled")
        pattern = sem("pattern")
        centred = sem("centred")
        squared = sem("squared")
        variance = sem("variance")
        deviated = sem("deviated")
        normed = sem("normed")
        stored = sem("stored")
        turned = sem("turned")
        turned_kept = sem("turned_kept")
        product = sem("product")
        product_kept = sem("product_kept")
        hidden = sem("hidden")
        hidden_kept = sem("hidden_kept")
        node_done = sem("node_done")
        stage_in = [sem(f"stage_in{k}") for k in range(2)]
        packed_a = sem("packed_a")
        packed_b = sem("packed_b")
        scattered = [sem(f"scattered{k}") for k in range(2)]
        scatter_go = sem("scatter_go")
        rec_ready = [sem(f"rec_ready{k}") for k in range(GPI)]
        gather_go = sem("gather_go")
        passed_t = sem("passed_t")
        passed_v = sem("passed_v")
        gathered = [sem(f"gathered{k}") for k in range(GPI)]
        fields = sem("fields")
        hot = sem("hot")
        summed = sem("summed")
        added = sem("added")
        attrT = sem("attrT")
        attrT_kept = sem("attrT_kept")
        edge_mm = sem("edge_mm")
        edge_used = sem("edge_used")
        edge_act = sem("edge_act")
        edge_mm2 = sem("edge_mm2")
        logits = sem("logits")
        gate_ready = sem("gate_ready")
        gate1 = sem("gate1")

        def dyn(start, n):
            return bass.ds(start, n)

        sort_ctx = ExitStack()
        with sort_ctx:
            def tmp(name, shape, dt=F32):
                return sbuf(name, shape, dt, sort_ctx)
            dst_i = tmp("dst_i", [P, COLS], I32)
            src_i = tmp("src_i", [P, COLS], I32)
            blk_i = tmp("blk_i", [P, COLS], I32)
            blk_f = tmp("blk_f", [P, COLS])
            lane_f = tmp("lane_f", [P, COLS])
            mask = tmp("mask", [P, COLS])
            ones_c = tmp("ones_c", [P, COLS])
            rank = tmp("rank", [P, COLS])
            pos = tmp("pos", [P, COLS])
            slot_i = tmp("slot_i", [P, COLS], I32)
            count = tmp("count", [P, NB])
            before = tmp("before", [P, P])
            ones_p = tmp("ones_p", [P, P])
            offs = tmp("offs", [P, NB])
            tiles_i = tmp("tiles_i", [P, NB], I32)
            tiles_f = tmp("tiles_f", [P, NB])
            t_end = tmp("t_end", [P, NB])
            t_start = tmp("t_start", [P, NB])
            start_col = tmp("start_col", [NB, 1])
            diag = tmp("diag", [NB, NB])
            tile_no = tmp("tile_no", [NB, T])
            block_w = tmp("block_w", [NB, 1])
            FK = 12
            unused = tmp("unused", [P, FK, RW])
            st_a = tmp("st_a", [P, 2, SC // 2, EA])
            st_b = tmp("st_b", [P, 2, SC // 2, EB])
            rec = tmp("rec_out", [P, 2, SC // 2, RW])
            slot_ring = tmp("slot_ring", [P, 2, SC // 2], I32)
            PC = T // 4
            assert T % 4 == 0 and PC <= 512 and T % FK == 0

            with nc.psum_tensor("ps_sort", [P, 6, 512], F32) as ps, nc.Block("sort") as block:
                @block.sync
                def _(sp):
                    sp.wait_ge(vec.sem, 2)
                    for t, a in ((dst_i, dst_in), (src_i, src_in)):
                        lanes = a[0:(P - 1) * COLS].rearrange("(p j) -> p j", j=COLS)
                        last = a[(P - 1) * COLS:E].rearrange("(p j) -> p j", p=1)
                        sp.dma_start(t[0:96, :], lanes[0:96, :]).then_inc(loaded.sem, 16)
                        sp.dma_start(t[96:P - 1, :], lanes[96:P - 1, :]).then_inc(loaded.sem, 16)
                        sp.dma_start(t[P - 1:P, 0:LAST], last).then_inc(loaded.sem, 16)
                    sp.wait_ge(pattern.sem, 1)
                    sp.dma_start(
                        rec_h.rearrange("(p a k) w -> p a (k w)", p=P, k=FK),
                        unused[:, :, :].rearrange("p k w -> p (k w)").unsqueeze(1)
                        .to_broadcast([P, T // FK, FK * RW])).then_inc(filled.sem, 16)
                    sp.wait_ge(filled.sem, 16)

                @block.scalar
                def _(a):
                    a.wait_ge(vec.sem, 4)
                    loads = [
                        (x[:, 0:FULL, :], x_in[0:FULL * P, :].rearrange("(b p) d -> p b d", p=P)),
                        (x[0:REST, FULL, :], x_in[FULL * P:N, :]),
                        (w0[0:D, 0:D], w["L0_gnn_W"]), (w0[D:D + 1, 0:D], w["L0_gnn_b"]),
                        (w1n[:, 0:D], w["L1_gnn_mW1"][0:D, :]), (w1n[:, D:2 * D], w["L1_gnn_gW1"][0:D, :]),
                        (w1e[0:EA, 0:D], w["L1_gnn_mW1"][D:D + EA, :]),
                        (w1e[0:EA, D:2 * D], w["L1_gnn_gW1"][D:D + EA, :]),
                        (w1e[EA:KA, 0:D], w["L1_gnn_mb1"]), (w1e[EA:KA, D:2 * D], w["L1_gnn_gb1"]),
                        (w2m[0:D, :], w["L1_gnn_mW2"]), (w2m[D:D + 1, :], w["L1_gnn_mb2"]),
                        (gw2[:, :], w["L1_gnn_gW2"].to_broadcast([P, D])),
                        (gb2[:, :], w["L1_gnn_gb2"].to_broadcast([P, 1])),
                        (u1x[:, :], w["L1_gnn_uW1"][0:D, :]), (u1a[:, :], w["L1_gnn_uW1"][D:2 * D, :]),
                        (ub1[:, :], w["L1_gnn_ub1"]),
                        (u2[0:D, :], w["L1_gnn_uW2"]), (u2[D:D + 1, :], w["L1_gnn_ub2"]),
                        (lng[:, :], w["L1_gnn_ln_g"].to_broadcast([P, D])),
                        (lnb[:, :], w["L1_gnn_ln_b"].to_broadcast([P, D])),
                        (w17[0:EB, :], w["L2_gnn_W1"]), (w17[EB:KB, :], w["L2_gnn_b1"]),
                        (w2w[0:D, :], w["L2_gnn_W2"]), (w2w[D:D + 1, :], w["L2_gnn_b2"]),
                        (wsT[0:D, :], w["L2_gnn_Ws"]), (wsT[D:D + 1, :], w["L2_gnn_bs"]),
                        (bn_row[D:D + 1, :], w["L2_gnn_bn"]), (wnT[:, :], w["L2_gnn_Wn"]),
                        (winT[0:D, :], w["L3_gnn_W_in"]), (winT[D:D + 1, :], w["L3_gnn_b_in"]),
                        (gcnT[:, :, :], w["L3_gnn_gcn_W"]),
                        (gcnb[:, :, :], w["L3_gnn_gcn_b"].unsqueeze(0).to_broadcast([P, 3, D])),
                        (woutT[0:D, :], w["L3_gnn_W_out"]), (woutT[D:D + 1, :], w["L3_gnn_b_out"]),
                    ]
                    for dst, src in loads:
                        a.dma_start(dst, src).then_inc(stored.sem, 16)
                    a.wait_ge(stored.sem, 16 * len(loads))
                    stored.n = 16 * len(loads)

                @block.gpsimd
                def _(g):
                    g.iota(iota[:, :], [[1, P]], base=0, channel_multiplier=0,
                           allow_small_or_imprecise_dtypes=True).then_inc(made.sem, 1)
                    g.iota(tile_no[:, :], [[1, T]], base=0, channel_multiplier=0,
                           allow_small_or_imprecise_dtypes=True).then_inc(made.sem, 1)
                    g.memset(ident[:, :], 0.0).then_inc(made.sem, 1)
                    g.memset(ones_p[:, :], 1.0).then_inc(made.sem, 1)
                    g.memset(before[:, :], 1.0).then_inc(made.sem, 1)
                    g.wait_ge(made.sem, 5)
                    g.affine_select(out=ident[:, :], in_=ident[:, :], compare_op=ALU.not_equal, fill=1.0,
                                    base=0, pattern=[[-1, P]], channel_multiplier=1).then_inc(made.sem, 1)
                    g.affine_select(out=before[:, :], in_=before[:, :], compare_op=ALU.is_gt, fill=0.0,
                                    base=0, pattern=[[1, P]], channel_multiplier=-1).then_inc(made.sem, 1)
                    g.memset(block_w[:, :], float(P)).then_inc(made.sem, 1)
                MADE = 8

                @block.vector
                def _(v):
                    chain(v, vec, v.memset(dst_i[:, :], NP - 1))
                    chain(v, vec, v.memset(src_i[:, :], 0))
                    chain(v, vec, v.memset(x[:, FULL:NB, :], 0.0))
                    chain(v, vec, v.memset(w0[:, D:D + 1], 0.0))
                    chain(v, vec, v.memset(unused[:, :, :], 0.0))
                    v.memset(unused[:, :, R_LANE:R_LANE + 1], -1.0).then_inc(pattern.sem, 1)
                    chain(v, vec, v.memset(w0[D:D + 1, D:D + 1], 1.0))
                    chain(v, vec, v.memset(ones_c[:, :], 1.0))
                    chain(v, vec, v.memset(rec[:, :, :, :], 1.0))
                    chain(v, vec, v.memset(st_a[:, :, :, :], 0.0))
                    chain(v, vec, v.memset(st_b[:, :, :, :], 0.0))
                    v.wait_ge(loaded.sem, 96)
                    chain(v, vec, v.tensor_scalar(blk_i[:, :], dst_i[:, :], 127, None, ALU.bitwise_and))
                    chain(v, vec, v.tensor_copy(lane_f[:, :], blk_i[:, :]))
                    chain(v, vec, v.tensor_scalar(blk_i[:, :], dst_i[:, :], 7, None, ALU.logical_shift_right))
                    chain(v, vec, v.tensor_copy(blk_f[:, :], blk_i[:, :]))
                    v.wait_ge(made.sem, MADE)
                    n0 = vec.n
                    with v.Fori(0, NB) as b:
                        v.tensor_scalar(mask[:, :], blk_f[:, :], iota[:, dyn(b, 1)], None, ALU.is_equal,
                                        ALU.add, accum_out=count[:, dyn(b, 1)]).then_inc(vec.sem, 1)
                        v.wait_ge(vec.sem, n0 + b + 1)
                    vec.n = n0 + NB
                    v.wait_ge(vec.sem, vec.n)
                    chain(v, counted, v.tensor_copy(count[:, :], count[:, :]))
                    v.wait_ge(offsets.sem, 1)
                    chain(v, vec, v.tensor_scalar(tiles_f[:, :], ps[:, 1, 0:NB], float(P - 1), None, ALU.add))
                    chain(v, vec, v.tensor_copy(tiles_i[:, :], tiles_f[:, :]))
                    chain(v, vec, v.tensor_scalar(tiles_i[:, :], tiles_i[:, :], 7, None, ALU.logical_shift_right))
                    chain(v, vec, v.tensor_copy(tiles_f[:, :], tiles_i[:, :]))
                    chain(v, vec, v.tensor_tensor_scan(t_end[:, :], ones_c[:, 0:NB], tiles_f[:, :], 0.0,
                                                       ALU.mult, ALU.add))
                    chain(v, vec, v.tensor_tensor(t_start[:, :], t_end[:, :], tiles_f[:, :], ALU.subtract))
                    chain(v, vec, v.scalar_tensor_tensor(out=offs[:, :], in0=t_start[:, :], scalar=float(P),
                                                         in1=ps[:, 0, 0:NB], op0=ALU.mult, op1=ALU.add))
                    chain(v, vec, v.tensor_tensor(diag[:, :], ident[0:NB, 0:NB], t_start[0:NB, :], ALU.mult))
                    chain(v, vec, v.reduce_sum(start_col[:, :], diag[:, :], AX.X))
                    chain(v, vec, v.tensor_scalar(tile_no[:, :], tile_no[:, :], start_col[:, 0:1], None,
                                                  ALU.is_ge))
                    v.tensor_copy(diag[:, :], diag[:, :]).then_inc(steps_up.sem, 1)
                    v.wait_ge(columns.sem, 1)
                    for c in range(4):
                        chain(v, vec, v.tensor_scalar(tile_col[:, c * PC:(c + 1) * PC], ps[0:1, 2 + c, 0:PC],
                                                      -float(P), None, ALU.add))
                    n0 = vec.n
                    with v.Fori(0, NB) as b:
                        v.tensor_scalar(mask[:, :], blk_f[:, :], iota[:, dyn(b, 1)], None,
                                        ALU.is_equal).then_inc(vec.sem, 1)
                        v.wait_ge(vec.sem, n0 + b * 3 + 1)
                        v.tensor_tensor_scan(rank[:, :], ones_c[:, :], mask[:, :], offs[:, dyn(b, 1)],
                                             ALU.mult, ALU.add).then_inc(vec.sem, 1)
                        v.wait_ge(vec.sem, n0 + b * 3 + 2)
                        v.sem_inc(passed_v.sem, 1)
                        v.copy_predicated(pos[:, :], mask[:, :].bitcast(I32), rank[:, :]).then_inc(vec.sem, 1)
                        v.wait_ge(vec.sem, n0 + b * 3 + 3)
                    vec.n = n0 + 3 * NB
                    v.wait_ge(vec.sem, vec.n)
                    chain(v, vec, v.tensor_scalar(pos[:, :], pos[:, :], -1.0, None, ALU.add))
                    chain(v, vec, v.tensor_copy(blk_i[:, :], pos[:, :]))
                    lane4, tile4 = mask[:, :].bitcast(I32), rank[:, :].bitcast(I32)
                    chain(v, vec, v.tensor_scalar(slot_i[:, :], blk_i[:, :], -(G * P), None, ALU.bitwise_and))
                    chain(v, vec, v.tensor_scalar(lane4, blk_i[:, :], P - 1, 2, ALU.bitwise_and,
                                                  ALU.logical_shift_left))
                    chain(v, vec, v.tensor_scalar(tile4, blk_i[:, :], 7, G - 1, ALU.logical_shift_right,
                                                  ALU.bitwise_and))
                    chain(v, vec, v.tensor_tensor(slot_i[:, :], slot_i[:, :], lane4, ALU.bitwise_or))
                    chain(v, vec, v.tensor_tensor(slot_i[:, :], slot_i[:, :], tile4, ALU.bitwise_or))

                @block.tensor
                def _(pe):
                    pe.wait_ge(made.sem, MADE)
                    pe.wait_ge(counted.sem, 1)
                    pe.matmul(ps[:, 0, 0:NB], before[:, :], count[:, :], start=True, stop=True)
                    pe.matmul(ps[:, 1, 0:NB], ones_p[:, :], count[:, :], start=True,
                              stop=True).then_inc(offsets.sem, 1)
                    pe.wait_ge(steps_up.sem, 1)
                    for c in range(4):
                        last = pe.matmul(ps[0:1, 2 + c, 0:PC], block_w[:, :], tile_no[:, c * PC:(c + 1) * PC],
                                         start=True, stop=True)
                    last.then_inc(columns.sem, 1)

            HC = SC // 2
            with nc.Block("scatter") as block:
                a_rows = e32[0:(P - 1) * COLS, :].rearrange("(p j) c -> p j c", j=COLS)
                b_rows = e17[0:(P - 1) * COLS, :].rearrange("(p j) c -> p j c", j=COLS)
                LT = LAST // SC
                ST = COLS // SC

                def both(eng, body):
                    for k in range(2):
                        body(0, k)
                    with eng.Fori(1, ST) as i:
                        for k in range(2):
                            body(i, k)

                @block.sync
                def _(sp):
                    def load(i, k, last):
                        col = i * SC + k * HC
                        sp.wait_ge(packed_a.sem, i * 2 + k + 1)
                        sp.wait_ge(packed_b.sem, i * 2 + k + 1)
                        for st, rows, flat in ((st_a, a_rows, e32), (st_b, b_rows, e17)):
                            sp.dma_start(st[0:96, k], rows[0:96, dyn(col, HC), :]).then_inc(stage_in[k].sem, 16)
                            sp.dma_start(st[96:P - 1, k],
                                         rows[96:P - 1, dyn(col, HC), :]).then_inc(stage_in[k].sem, 16)
                            if last:
                                sp.dma_start(st[P - 1:P, k].rearrange("p j c -> p (j c)"),
                                             flat[dyn(col + (P - 1) * COLS, HC), :]
                                             .rearrange("(o j) c -> o (j c)", o=1)).then_inc(stage_in[k].sem, 16)
                            else:
                                sp.sem_inc(stage_in[k].sem, 16)
                    with sp.Fori(0, LT) as i:
                        load(i, 0, True)
                        load(i, 1, True)
                    with sp.Fori(LT, ST) as i:
                        load(i, 0, False)
                        load(i, 1, False)

                @block.scalar
                def _(a):
                    a.sem_inc(packed_a.sem, 2)
                    def body(i, k):
                        a.wait_ge(stage_in[k].sem, (i + 1) * 96)
                        wait_past(a, scattered[k].sem, 0, i * (16 * HC))
                        a.activation(rec[:, k, :, R_A:R_A + EA], st_a[:, k], ACT.Copy).then_inc(packed_a.sem, 1)
                    both(a, body)

                @block.vector
                def _(v):
                    v.sem_inc(packed_b.sem, 2)
                    n0 = vec.n
                    def body(i, k):
                        cols = dyn(i * SC + k * HC, HC)
                        v.wait_ge(stage_in[k].sem, (i + 1) * 96)
                        wait_past(v, scattered[k].sem, 0, i * (16 * HC))
                        v.tensor_copy(rec[:, k, :, R_B:R_B + EB], st_b[:, k])
                        v.tensor_copy(rec[:, k, :, R_SRC].bitcast(I32), src_i[:, cols])
                        v.tensor_copy(rec[:, k, :, R_LANE], lane_f[:, cols])
                        v.tensor_copy(slot_ring[:, k, :], slot_i[:, cols]).then_inc(packed_b.sem, 1)
                    both(v, body)

                @block.gpsimd
                def _(g):
                    def body(i, k):
                        g.wait_ge(packed_a.sem, i * 2 + k + 3)
                        g.wait_ge(packed_b.sem, i * 2 + k + 3)
                        g.sem_inc(scatter_go.sem, 1)
                        for j in range(HC):
                            g.indirect_dma_start(
                                out=rec_h, out_offset=bass.IndirectOffsetOnAxis(ap=slot_ring[:, k, j:j + 1], axis=0),
                                in_=rec[:, k, j, :], in_offset=None).then_inc(scattered[k].sem, 16)
                    both(g, body)
                    for k in range(2):
                        g.wait_ge(scattered[k].sem, ST * 16 * HC)

        hT = sbuf("hT", [D + 1, NP])
        wide = sbuf("wide", [P, GB, 2 * D])
        part = sbuf("part", [P, GB, D])
        part2 = sbuf("part2", [P, GB])
        aggT = sbuf("aggT", [D, GB * P])
        uT = sbuf("uT", [D + 1, GB * P])
        with nc.Block("ones") as block:
            @block.gpsimd
            def _(g):
                g.memset(hT[D:D + 1, :], 1.0).then_inc(made.sem, 1)
                g.memset(uT[D:D + 1, :], 1.0).then_inc(made.sem, 1)

            @block.vector
            def _(v):
                v.tensor_tensor(wsT[D:D + 1, :], wsT[D:D + 1, :], bn_row[D:D + 1, :], ALU.add).then_inc(vec.sem, 1)
                vec.n += 1
                v.tensor_scalar(half_gb2[:, :], gb2[:, :], 0.5, None, ALU.mult).then_inc(vec.sem, 1)
                vec.n += 1
                v.wait_ge(vec.sem, vec.n)

        def rows_bc(t):
            return t[:, :].unsqueeze(2).to_broadcast([P, NB, D])

        def norm_steps(block, src, dst, sq, finish, n_done=1):
            @block.vector
            def _(v):
                chain(v, vec, v.reduce_sum(s_sum[:, :], src[:, :, :], AX.X))
                chain(v, vec, v.tensor_scalar(s_sum[:, :], s_sum[:, :], 1.0 / D, None, ALU.mult))
                chain(v, centred, v.tensor_tensor(dst[:, :, :], src[:, :, :], rows_bc(s_sum), ALU.subtract))
                v.wait_ge(squared.sem, centred.n)
                chain(v, vec, v.reduce_sum(s_var[:, :], sq[:, :, :], AX.X))
                chain(v, variance, v.tensor_scalar(s_var[:, :], s_var[:, :], 1.0 / D, EPS, ALU.mult, ALU.add))
                v.wait_ge(deviated.sem, centred.n)
                chain(v, vec, v.reciprocal(s_rstd[:, :], s_std[:, :]))
                finish(v)

            @block.scalar
            def _(a):
                k = squared.n + 1
                a.wait_ge(centred.sem, k)
                a.activation(sq[:, :, :], dst[:, :, :], ACT.Square).then_inc(squared.sem, 1)
                a.wait_ge(variance.sem, k)
                a.activation(s_std[:, :], s_var[:, :], ACT.Sqrt).then_inc(deviated.sem, 1)
                squared.n = deviated.n = k

        def norm_relu(table):
            with nc.Block() as block, nc.sbuf_tensor(nc_name("sq"), [P, NB, D], F32) as sq:
                def finish(v):
                    chain(v, normed, v.scalar_tensor_tensor(out=h[:, :, :], in0=h[:, :, :], scalar=0.0,
                                                            in1=rows_bc(s_rstd), op0=ALU.max, op1=ALU.mult))
                norm_steps(block, x, h, sq, finish)

                @block.gpsimd
                def _(g):
                    g.memset(accT[:, :], 0.0).then_inc(made.sem, 1)
                if table:
                    @block.sync
                    def _(sp):
                        sp.wait_ge(normed.sem, normed.n)
                        sp.dma_start(tab_v, h[:, :, :]).then_inc(stored.sem, 16)
                        stored.n += 16
                        sp.wait_ge(stored.sem, stored.n)

        names = [0]

        def nc_name(s):
            names[0] += 1
            return f"{s}_{names[0]}"

        def transpose_nodes(src, dstT):
            with nc.psum_tensor(nc_name("psT"), [P, 2, 4, P], F32) as ps, nc.Block() as block:
                flat = ps[:, :, :, :].rearrange("p a b c -> p (a b c)")
                t0, k0 = turned.n, turned_kept.n

                @block.tensor
                def _(pe):
                    for s in range(GS):
                        pe.wait_ge(turned_kept.sem, s + k0)
                        for j in range(GB):
                            last = pe.transpose(ps[0:D, j // 4, j % 4, :],
                                                src[:, s * GB + j, :],
                                                ident[:, :])
                        last.then_inc(turned.sem, 1)

                @block.scalar
                def _(a):
                    with a.Fori(0, GS) as s:
                        a.wait_ge(turned.sem, s + (t0 + 1))
                        a.activation(dstT[0:D, dyn(s * (GB * P), GB * P)], flat[0:D, 0:GB * P],
                                     ACT.Copy).then_inc(turned_kept.sem, 1)
                turned.n += GS
                turned_kept.n += GS

        def node_product(terms, width, reader, use_scalar=False, extra=None):
            per = 1 if width > P else 4
            banks = -(-GB // (2 if width > P else 4))
            pitch = 512 // (2 if width > P else 4)
            with nc.psum_tensor(nc_name("psN"), [P, banks * 512 // pitch, pitch], F32) as ps, \
                    nc.Block() as block:
                p0, k0 = product.n, product_kept.n

                @block.tensor
                def _(pe):
                    for s in range(GS):
                        pe.wait_ge(product_kept.sem, s + k0)
                        for j in range(GB):
                            for n, (rowsT, k, wt) in enumerate(terms):
                                last = pe.matmul(ps[:, j, 0:width], rowsT[0:k, (s * GB + j) * P:(s * GB + j + 1) * P], wt,
                                                 start=(n == 0), stop=(n == len(terms) - 1))
                        last.then_inc(product.sem, 1)

                reader(block, ps, p0)
                if extra:
                    extra(block)
                product.n += GS
                product_kept.n += GS

        def edge_pass(kind, table, width, first=False):
            recs = kind != "copy" or first
            ctx = ExitStack()
            with ctx:
                def tmp(name, shape, dt=F32):
                    return sbuf(nc_name(name), shape, dt, ctx)

                def psum(name, shape):
                    return ctx.enter_context(nc.psum_tensor(nc_name(name), shape, F32))
                gw = width + 1 if first else width
                M = D + 1 if (first or kind == "gated") else D
                rows = tmp("rows", [P, GPI, G, gw])
                hots = tmp("hots", [P, 2, G, P])
                ps_sum = psum("ps_sum", [P, 2, G, P])
                if recs:
                    ring = tmp("rec_ring", [P, GPI, G * RW])
                    ring_v = ring[:, :, :].rearrange("p s (j w) -> p s j w", j=G)
                else:
                    idx_ring = tmp("idx_ring", [P, GPI, G], I32)
                if kind == "gated":
                    ps_t = psum("ps_t", [P, 2, 512])
                    ps_e = psum("ps_e", [P, 2, 2, 512])
                    aT = tmp("aT", [KA, 2, 512])
                    act_ring = tmp("act_ring", [P, 3, G, 2, D + 1])
                    z = tmp("z", [P, 3, G])
                    th = tmp("th", [P, 3, G])
                    gate = tmp("gate", [P, 3, G])
                if kind == "filter":
                    ps_t = psum("ps_t", [P, 2, 512])
                    ps_e = psum("ps_e", [P, 2, 512])
                    ps_w = psum("ps_w", [P, 2, G, P])
                    aT = tmp("aT", [KB, 2, 512])
                    hid = tmp("hid", [D + 1, 2, 512])
                    msg = tmp("msg", [P, 3, G, D])

                base = {s: s.n for s in (rec_ready + gathered + [gather_go, fields, hot, summed, added,
                                                                attrT, attrT_kept, edge_mm, edge_used, edge_act,
                                                                edge_mm2, logits, gate_ready, gate1])}
                rows_used = summed if kind == "copy" else edge_used
                block = ctx.enter_context(nc.Block())

                def past(eng, sig, q):
                    wait_past(eng, sig.sem, base[sig], q)

                @block.sync
                def _(sp):
                    def load(q, turn, r):
                        past(sp, rows_used, q - (GPI - 1))
                        if recs:
                            if first:
                                past(sp, fields, q - (GPI - 1))
                            src = rec_groups[dyn(q, 1), :, :].rearrange("o p w -> (o p) w")
                            sp.dma_start(ring[:, r, :], src).then_inc(rec_ready[r].sem, 16)
                        else:
                            sp.dma_start(idx_ring[:, r, :], src_all[:, dyn(q * G, G)]).then_inc(rec_ready[r].sem, 16)
                    turns(sp, [(load, 0)])

                @block.gpsimd
                def _(g):
                    if first:
                        g.memset(rows[:, :, :, D:D + 1], 1.0).then_inc(made.sem, 1)
                    if kind == "gated":
                        g.memset(act_ring[:, :, :, 0, D:D + 1], 1.0).then_inc(made.sem, 1)
                    if kind == "filter":
                        g.memset(hid[D:D + 1, :, :], 1.0).then_inc(made.sem, 1)

                    def gather(q, turn, r):
                        g.wait_ge(rec_ready[r].sem, base[rec_ready[r]] + (turn + 1) * 16)
                        g.sem_inc(gather_go.sem, 1)
                        for j in range(G):
                            idx = ring_v[:, r, j, R_SRC:R_SRC + 1].bitcast(I32) if recs else idx_ring[:, r, j:j + 1]
                            g.indirect_dma_start(
                                out=rows[:, r, j, 0:width], out_offset=None, in_=table,
                                in_offset=bass.IndirectOffsetOnAxis(ap=idx, axis=0)).then_inc(gathered[r].sem, 16)
                    turns(g, [(gather, 0)])
                made.n += 1 if (first or kind != "copy") else 0

                def rows_in(eng, turn, r):
                    eng.wait_ge(gathered[r].sem, base[gathered[r]] + (turn + 1) * (16 * G))

                def hots_and_adds(v, with_hots, with_adds):
                    if with_adds:
                        qa, _, ra = with_adds
                        cols = nc.values_load_multi_w_load_instructions(
                            tile_col[0:1, dyn(qa * G, G)], [DVE], min_val=0, max_val=(NB - 1) * P,
                            skip_runtime_bounds_check_because="columns of the blocks, at most the last block's")[1]
                        past(v, summed, qa + 1)
                    if with_hots:
                        q, _, r = with_hots
                        if first:
                            past(v, fields, q + 1)
                        if kind == "gated":
                            past(v, gate_ready, q + 1)
                            v.tensor_scalar(gate[:, r % 3, :], th[:, r % 3, :], 1.0, None,
                                            ALU.add).then_inc(gate1.sem, 1)
                            past(v, gate1, q + 1)
                        past(v, summed, q - 1)
                    for j in range(G):
                        if with_hots:
                            lane = lane_all[:, dyn(q * G + j, 1)]
                            if kind == "gated":
                                last = v.tensor_scalar(hots[:, r % 2, j, :], iota[:, :], lane,
                                                       gate[:, r % 3, j:j + 1], ALU.is_equal, ALU.mult)
                            else:
                                last = v.tensor_scalar(hots[:, r % 2, j, :], iota[:, :], lane, None, ALU.is_equal)
                            if j == G - 1:
                                last.then_inc(hot.sem, 1)
                        if with_adds:
                            past(v, added, qa * G + j)
                            acc = accT[0:M, dyn(cols[j], P)]
                            v.tensor_tensor(acc, acc, ps_sum[0:M, ra % 2, j, :], ALU.add).then_inc(added.sem, 1)

                def sum_targets(pe, q, turn, r, what):
                    past(pe, hot, q + 1)
                    past(pe, added, (q - 1) * G)
                    for j in range(G):
                        last = pe.matmul(ps_sum[0:M, r % 2, j, :], what(r, j), hots[:, r % 2, j, :],
                                         start=True, stop=True)
                    last.then_inc(summed.sem, 1)

                def transposes(pe, q, turn, r, c0, kk):
                    pe.wait_ge(rec_ready[r].sem, base[rec_ready[r]] + (turn + 1) * 16)
                    past(pe, attrT_kept, q - 1)
                    pe.sem_inc(passed_t.sem, 1)
                    for j in range(G):
                        last = pe.transpose(ps_t[0:kk, r % 2, j * P:(j + 1) * P], ring_v[:, r, j, c0:c0 + kk],
                                            ident[:, :])
                    last.then_inc(attrT.sem, 1)

                def keep_attrT(a, q, turn, r, kk, free):
                    past(a, attrT, q + 1)
                    past(a, free, q - 1)
                    a.activation(aT[:, r % 2, :], ps_t[0:kk, r % 2, :], ACT.Copy).then_inc(attrT_kept.sem, 1)

                if kind == "copy":
                    @block.tensor
                    def _(pe):
                        def work(q, turn, r):
                            rows_in(pe, turn, r)
                            sum_targets(pe, q, turn, r, lambda r, j: rows[:, r, j, 0:M])
                        if first:
                            pe.wait_ge(made.sem, made.n)
                        turns(pe, [(work, 0)])

                    @block.vector
                    def _(v):
                        turns(v, [(lambda new, old: hots_and_adds(v, new, old), 0, 1)])
                    if first:
                        @block.scalar
                        def _(a):
                            def keep(q, turn, r):
                                a.wait_ge(rec_ready[r].sem, base[rec_ready[r]] + (turn + 1) * 16)
                                a.activation(src_all[:, dyn(q * G, G)], ring_v[:, r, :, R_SRC].bitcast(I32), ACT.Copy)
                                a.activation(lane_all[:, dyn(q * G, G)], ring_v[:, r, :, R_LANE],
                                             ACT.Copy).then_inc(fields.sem, 1)
                            turns(a, [(keep, 0)])

                if kind == "gated":
                    @block.tensor
                    def _(pe):
                        pe.wait_ge(made.sem, made.n)

                        def edge_part(q, turn, r):
                            past(pe, attrT_kept, q + 1)
                            past(pe, edge_used, q - 1)
                            for j in range(G):
                                last = pe.matmul(ps_e[:, r % 2, j // 2, (j % 2) * 2 * D:(j % 2 + 1) * 2 * D],
                                                 aT[:, r % 2, j * P:(j + 1) * P], w1e[:, :], start=True, stop=True)
                            last.then_inc(edge_mm.sem, 1)
                        turns(pe, [(lambda q, t, r: transposes(pe, q, t, r, R_A, KA), 0), (edge_part, 1),
                                   (lambda q, t, r: sum_targets(pe, q, t, r,
                                                                lambda r, j: act_ring[:, r % 3, j, 0, :]), 4)])

                    @block.scalar
                    def _(a):
                        def gelu(q, turn, r):
                            past(a, edge_used, q + 1)
                            v4 = act_ring[:, r % 3, :, :, 0:D].rearrange("p j a d -> p (j a) d")
                            a.activation(v4, v4, ACT.Gelu).then_inc(edge_act.sem, 1)

                        def tanh(q, turn, r):
                            past(a, logits, q + 1)
                            past(a, gate1, q - 2)
                            a.activation(th[:, r % 3, :], z[:, r % 3, :], ACT.Tanh, bias=half_gb2[:, 0:1],
                                         scale=0.5).then_inc(gate_ready.sem, 1)
                        turns(a, [(lambda q, t, r: keep_attrT(a, q, t, r, KA, edge_mm), 0), (gelu, 2), (tanh, 3)])

                    @block.vector
                    def _(v):
                        def combine(q, turn, r):
                            rows_in(v, turn, r)
                            past(v, edge_mm, q + 1)
                            past(v, summed, q - 2)
                            for c in range(2):
                                last = v.tensor_tensor(
                                    act_ring[:, r % 3, 2 * c:2 * c + 2, :, 0:D].rearrange("p j a d -> p (j a) d"),
                                    ps_e[:, r % 2, c, 0:4 * D].rearrange("p (j d) -> p j d", d=D),
                                    rows[:, r, 2 * c:2 * c + 2, :].rearrange("p j (a d) -> p (j a) d", d=D), ALU.add)
                            last.then_inc(edge_used.sem, 1)

                        def dots(q, turn, r):
                            past(v, edge_act, q + 1)
                            for j in range(G):
                                last = v.tensor_tensor_reduce(out=act_ring[:, r % 3, j, 1, 0:D], in0=act_ring[:, r % 3, j, 1, 0:D],
                                                              in1=gw2[:, :], scale=1.0, scalar=0.0, op0=ALU.mult,
                                                              op1=ALU.add, accum_out=z[:, r % 3, j:j + 1])
                            last.then_inc(logits.sem, 1)

                        turns(v, [(lambda new, old: hots_and_adds(v, new, old), 4, 5), (combine, 2), (dots, 3)])

                if kind == "filter":
                    @block.tensor
                    def _(pe):
                        pe.wait_ge(made.sem, made.n)

                        def layer1(q, turn, r):
                            past(pe, attrT_kept, q + 1)
                            past(pe, edge_act, q - 1)
                            pe.matmul(ps_e[0:D, r % 2, :], w17[:, :], aT[:, r % 2, :], start=True,
                                      stop=True).then_inc(edge_mm.sem, 1)

                        def layer2(q, turn, r):
                            past(pe, edge_act, q + 1)
                            past(pe, edge_used, q - 1)
                            for j in range(G):
                                last = pe.matmul(ps_w[:, r % 2, j, 0:D], hid[:, r % 2, j * P:(j + 1) * P], w2w[:, :],
                                                 start=True, stop=True)
                            last.then_inc(edge_mm2.sem, 1)
                        turns(pe, [(lambda q, t, r: transposes(pe, q, t, r, R_B, KB), 0), (layer1, 1), (layer2, 2),
                                   (lambda q, t, r: sum_targets(pe, q, t, r, lambda r, j: msg[:, r % 3, j, :]), 4)])

                    @block.scalar
                    def _(a):
                        def relu(q, turn, r):
                            past(a, edge_mm, q + 1)
                            past(a, edge_mm2, q - 1)
                            a.activation(hid[0:D, r % 2, :], ps_e[0:D, r % 2, :], ACT.Relu).then_inc(edge_act.sem, 1)
                        turns(a, [(lambda q, t, r: keep_attrT(a, q, t, r, KB, edge_mm), 0), (relu, 1)])

                    @block.vector
                    def _(v):
                        def times(q, turn, r):
                            rows_in(v, turn, r)
                            past(v, edge_mm2, q + 1)
                            past(v, summed, q - 2)
                            v.tensor_tensor(msg[:, r % 3, :, :], ps_w[:, r % 2, :, 0:D], rows[:, r, :, :],
                                            ALU.mult).then_inc(edge_used.sem, 1)
                        turns(v, [(lambda new, old: hots_and_adds(v, new, old), 4, 5), (times, 3)])

                for s in rec_ready:
                    s.n += 16 * TURNS
                for s in gathered:
                    s.n += 16 * G * TURNS
                for s in (gather_go, hot, summed):
                    s.n += Q
                added.n += T
                if first:
                    fields.n += Q
                if kind != "copy":
                    for s in (attrT, attrT_kept, edge_mm, edge_used, edge_act):
                        s.n += Q
                if kind == "filter":
                    edge_mm2.n += Q
                if kind == "gated":
                    for s in (logits, gate_ready, gate1):
                        s.n += Q

        made.n = 10
        blocks_of = lambda t, s: t[:, dyn(s * GB, GB), :]
        part_bc = lambda t, s: t[:, dyn(s * GB, GB)].unsqueeze(2).to_broadcast([P, GB, D])

        def vector_reader(steps, n_chain):
            def reader(block, ps, p0):
                @block.vector
                def _(v):
                    v0 = vec.n
                    with v.Fori(0, GS) as s:
                        v.wait_ge(product.sem, s + (p0 + 1))
                        k = [0]

                        def link(ins):
                            k[0] += 1
                            ins.then_inc(vec.sem, 1)
                            v.wait_ge(vec.sem, s * n_chain + (v0 + k[0]))
                        last = steps(v, s, ps, link)
                        assert k[0] == n_chain
                        last.then_inc(product_kept.sem, 1)
                    vec.n = v0 + n_chain * GS
            return reader

        def store(view, src):
            with nc.Block() as block:
                @block.sync
                def _(sp):
                    sp.dma_start(view, src).then_inc(stored.sem, 16)
                    stored.n += 16
                    sp.wait_ge(stored.sem, stored.n)

        norm_relu(True)
        made.n += 1
        edge_pass("copy", tab_h, D, first=True)

        def mean_update(v, s, ps, link):
            link(v.tensor_copy(part2[:, :], ps[:, 0:GB, D]))
            link(v.tensor_scalar(dinv[:, dyn(s * GB, GB)], part2[:, :], 1.0, None, ALU.add))
            link(v.tensor_scalar(part2[:, :], part2[:, :], 1.0, None, ALU.max))
            link(v.reciprocal(rdeg[:, dyn(s * GB, GB)], part2[:, :]))
            link(v.tensor_tensor(part[:, :, :], ps[:, 0:GB, 0:D], part_bc(rdeg, s), ALU.mult))
            return v.tensor_tensor(blocks_of(x, s), blocks_of(x, s), part[:, :, :], ALU.add)
        node_product([(accT, D + 1, w0[:, :])], D + 1, vector_reader(mean_update, 5))
        with nc.Block() as block:
            @block.scalar
            def _(a):
                a.activation(dinv[:, :], dinv[:, :], ACT.Sqrt).then_inc(act.sem, 1)

            @block.vector
            def _(v):
                v.wait_ge(act.sem, 1)
                v.reciprocal(dinv[:, :], dinv[:, :]).then_inc(vec.sem, 1)
                vec.n += 1
                v.wait_ge(vec.sem, vec.n)

        norm_relu(False)
        made.n += 1
        transpose_nodes(h, hT)

        def keep_wide(block, ps, p0):
            @block.scalar
            def _(a):
                s0 = stored.n
                with a.Fori(0, GS) as s:
                    a.wait_ge(product.sem, s + (p0 + 1))
                    a.wait_ge(stored.sem, s * 16 + s0)
                    a.activation(wide[:, :, :], ps[:, 0:GB, 0:2 * D], ACT.Copy).then_inc(product_kept.sem, 1)

            @block.sync
            def _(sp):
                k0, s0 = product_kept.n, stored.n
                with sp.Fori(0, GS) as s:
                    sp.wait_ge(product_kept.sem, s + (k0 + 1))
                    sp.dma_start(tab2_v[:, dyn(s * GB, GB), :], wide[:, :, :]).then_inc(stored.sem, 16)
                stored.n += 16 * GS
                sp.wait_ge(stored.sem, stored.n)
        node_product([(hT, D, w1n[:, :])], 2 * D, keep_wide)
        edge_pass("gated", tab2_h, 2 * D)

        with nc.psum_tensor("ps_agg", [P, 2, 512], F32) as ps_a, nc.psum_tensor("ps_hid", [P, 2, 512], F32) as ps_b, \
                nc.psum_tensor("ps_upd", [P, 8, P], F32) as ps_c, nc.Block() as block:
            cuts = ((0, 512), (512, GB * P))
            flat_a = ps_a[:, :, :].rearrange("p a b -> p (a b)")
            flat_b = ps_b[:, :, :].rearrange("p a b -> p (a b)")
            hidden_kept.n += 1
            t0, tk0, h0, hk0, p0, k0 = turned.n, turned_kept.n, hidden.n, hidden_kept.n, product.n, product_kept.n

            @block.tensor
            def _(pe):
                with pe.Fori(0, GS) as s:
                    col = s * (GB * P)
                    pe.wait_ge(turned_kept.sem, s + tk0)
                    for n, (lo, hi) in enumerate(cuts):
                        last = pe.matmul(ps_a[0:D, n, 0:hi - lo], w2m[:, :], accT[:, dyn(col + lo, hi - lo)],
                                         start=True, stop=True)
                    last.then_inc(turned.sem, 1)
                    pe.wait_ge(turned_kept.sem, s + (tk0 + 1))
                    pe.wait_ge(hidden_kept.sem, s + hk0)
                    for n, (lo, hi) in enumerate(cuts):
                        pe.matmul(ps_b[0:D, n, 0:hi - lo], u1x[:, :], hT[0:D, dyn(col + lo, hi - lo)],
                                  start=True, stop=False)
                        last = pe.matmul(ps_b[0:D, n, 0:hi - lo], u1a[:, :], aggT[:, lo:hi], start=False, stop=True)
                    last.then_inc(hidden.sem, 1)
                    pe.wait_ge(hidden_kept.sem, s + (hk0 + 1))
                    pe.wait_ge(product_kept.sem, s + k0)
                    for j in range(GB):
                        last = pe.matmul(ps_c[:, j, 0:D], uT[:, j * P:(j + 1) * P], u2[:, :], start=True, stop=True)
                    last.then_inc(product.sem, 1)

            @block.scalar
            def _(a):
                a.sem_inc(hidden_kept.sem, 1)
                with a.Fori(0, GS) as s:
                    a.wait_ge(turned.sem, s + (t0 + 1))
                    a.activation(aggT[:, :], flat_a[0:D, 0:GB * P], ACT.Copy, scale=0.5).then_inc(turned_kept.sem, 1)
                    a.wait_ge(hidden.sem, s + (h0 + 1))
                    a.activation(uT[0:D, :], flat_b[0:D, 0:GB * P], ACT.Gelu, bias=ub1[:, 0:1])\
                        .then_inc(hidden_kept.sem, 1)

            @block.vector
            def _(v):
                with v.Fori(0, GS) as s:
                    v.wait_ge(product.sem, s + (p0 + 1))
                    v.tensor_tensor(blocks_of(h, s), blocks_of(h, s), ps_c[:, 0:GB, 0:D], ALU.add)\
                        .then_inc(product_kept.sem, 1)
            for sig in (turned, turned_kept, hidden, hidden_kept, product, product_kept):
                sig.n += GS

        def over_d(t):
            return t[:, :].unsqueeze(1).to_broadcast([P, NB, D])
        with nc.Block() as block, nc.sbuf_tensor("sq_l1", [P, NB, D], F32) as sq:
            def finish(v):
                chain(v, vec, v.tensor_tensor(h[:, :, :], h[:, :, :], rows_bc(s_rstd), ALU.mult))
                chain(v, vec, v.tensor_tensor(h[:, :, :], h[:, :, :], over_d(lng), ALU.mult))
                chain(v, vec, v.tensor_tensor(h[:, :, :], h[:, :, :], over_d(lnb), ALU.add))
                chain(v, vec, v.tensor_tensor(x[:, :, :], x[:, :, :], h[:, :, :], ALU.add))
            norm_steps(block, h, h, sq, finish)

        norm_relu(True)
        made.n += 1
        transpose_nodes(h, hT)
        edge_pass("filter", tab_h, D)

        def relu_add(v, s, ps, link):
            return v.scalar_tensor_tensor(out=blocks_of(x, s), in0=ps[:, 0:GB, 0:D], scalar=0.0,
                                          in1=blocks_of(x, s), op0=ALU.max, op1=ALU.add)
        node_product([(hT, D + 1, wsT[:, :]), (accT, D, wnT[:, :])], D, vector_reader(relu_add, 0))

        norm_relu(False)
        made.n += 1
        transpose_nodes(h, hT)
        cur = h
        scaled = sbuf("scaled", [P, NB, D])

        def enter(v, s, ps, link):
            link(v.tensor_scalar(blocks_of(cur, s), ps[:, 0:GB, 0:D], 0.0, None, ALU.max))
            return v.tensor_tensor(blocks_of(scaled, s), blocks_of(cur, s), part_bc(dinv, s), ALU.mult)
        node_product([(hT, D + 1, winT[:, :])], D, vector_reader(enter, 1))
        for layer in range(3):
            store(tab_v, scaled[:, :, :])
            transpose_nodes(scaled, accT)
            edge_pass("copy", tab_h, D)

            def convolve(v, s, ps, link):
                link(v.tensor_tensor(part[:, :, :], ps[:, 0:GB, 0:D], part_bc(dinv, s), ALU.mult))
                link(v.tensor_tensor(part[:, :, :], part[:, :, :],
                                     gcnb[:, layer, :].unsqueeze(1).to_broadcast([P, GB, D]), ALU.add))
                link(v.scalar_tensor_tensor(out=blocks_of(cur, s), in0=part[:, :, :], scalar=0.0,
                                            in1=blocks_of(cur, s), op0=ALU.max, op1=ALU.add))
                return v.tensor_tensor(blocks_of(scaled, s), blocks_of(cur, s), part_bc(dinv, s), ALU.mult)
            node_product([(accT, D, gcnT[:, layer, :])], D, vector_reader(convolve, 3))
        transpose_nodes(cur, hT)

        def finish_x(v, s, ps, link):
            return v.tensor_tensor(blocks_of(x, s), ps[:, 0:GB, 0:D], blocks_of(x, s), ALU.add)
        node_product([(hT, D + 1, woutT[:, :])], D, vector_reader(finish_x, 0))
        with nc.Block() as block:
            @block.sync
            def _(sp):
                sp.dma_start(out_h[0:FULL * P, :].rearrange("(b p) d -> p b d", p=P), x[:, 0:FULL, :])\
                    .then_inc(stored.sem, 16)
                sp.dma_start(out_h[FULL * P:N, :], x[0:REST, FULL, :]).then_inc(stored.sem, 16)
                stored.n += 32
                sp.wait_ge(stored.sem, stored.n)


_TURNED = ("L2_gnn_W1", "L2_gnn_W2", "L2_gnn_Ws", "L2_gnn_Wn", "L3_gnn_W_in", "L3_gnn_W_out")
_COLUMN = ("L1_gnn_ub1",)


def kernel(**inputs):
    import numpy as _np
    import concourse.bacc as _bacc
    from concourse import mybir as _mybir
    from concourse.bass_utils import run_bass_kernel_spmd as _run

    nc = _bacc.Bacc("TRN2", target_bir_lowering=False, num_devices=1)
    arrays, aps = {}, {}
    for name, value in inputs.items():
        a = _np.asarray(value)
        if name in _TURNED:
            a = a.T
        elif name == "L3_gnn_gcn_W":
            a = a.transpose(2, 0, 1)
        elif name == "L1_gnn_gW2":
            a = a.reshape(1, D)
        elif name in _COLUMN:
            a = a.reshape(-1, 1)
        elif a.ndim == 1 and name not in ("src", "dst"):
            a = a.reshape(1, -1)
        a = _np.ascontiguousarray(a)
        arrays[f"in_{name}"] = a
        aps[name] = nc.dram_tensor(f"in_{name}", a.shape, _mybir.dt.from_np(a.dtype), kind="ExternalInput").ap()
    aps["out"] = nc.dram_tensor("out_x", (N, D), _mybir.dt.float32, kind="ExternalOutput").ap()
    graph_kernel(nc, aps["x"], aps["src"], aps["dst"], aps["edge_attr_17"], aps["edge_attr_32"], aps)
    r = _run(nc, [arrays], core_ids=[0])
    return r.results[0]["out_x"]
```

```python
import numpy as np
import concourse.bass as bass
from concourse import mybir
from contextlib import ExitStack

F32 = mybir.dt.float32
I32 = mybir.dt.int32
ALU = mybir.AluOpType
ACT = mybir.ActivationFunctionType
AX = mybir.AxisListType
SP, PE, DVE, POOL, ACTE = (mybir.EngineType.SP, mybir.EngineType.PE, mybir.EngineType.DVE,
                           mybir.EngineType.Pool, mybir.EngineType.Activation)

P = 128
N, D, E = 6250, 96, 200000
EA, EB = 32, 17
NB = -(-N // P)
NP = NB * P
FULL = N // P
REST = N - FULL * P

SC = 16
COLS = -(-(-(-E // P)) // SC) * SC
LAST = E - (P - 1) * COLS
PADDED = COLS * P
ROWS = PADDED + P
assert 0 < LAST <= COLS and LAST % SC == 0

G = 4
GPI = 6
TILES = (PADDED + NB * (P - 1)) // P
Q = -(-TILES // G)
T = Q * G

KA, KB = EA + 1, EB + 1

GB = 7
GS = NB // GB
EPS = 1e-5


class Signal:

    def __init__(self, ctx, nc, name):
        self.sem = ctx.enter_context(nc.semaphore(name))
        self.n = 0


def chain(eng, sig, ins):
    ins.then_inc(sig.sem, 1)
    sig.n += 1
    eng.wait_ge(sig.sem, sig.n)


def turns(eng, stages):
    def place(i, s, lag):
        q = i * GPI + (s - lag)
        if isinstance(i, int) and not 0 <= q < Q:
            return None
        return q, i if s >= lag else i - 1, (s - lag) % GPI

    def turn(i):
        for s in range(GPI):
            for work, *lags in stages:
                places = [place(i, s, lag) for lag in lags]
                if len(places) > 1 and any(places):
                    work(*places)
                elif places[0]:
                    work(*places[0])
    turn(0)
    with eng.Fori(1, Q // GPI) as i:
        turn(i)
    turn(Q // GPI)
    turn(Q // GPI + 1)


def wait_past(eng, sem, base, q):
    if isinstance(q, int) and q <= 0:
        return
    eng.wait_ge(sem, base + q)


def graph_kernel(nc, x_in, src_in, dst_in, e17, e32, w):
    out_h = w["out"]
    top = ExitStack()
    with top:
        def sem(name):
            return Signal(top, nc, name)

        def sbuf(name, shape, dt=F32, ctx=top):
            return ctx.enter_context(nc.sbuf_tensor(name, shape, dt))

        pairs_h = nc.dram_tensor("sorted_pairs", (ROWS, 2), I32, kind="Internal").ap()
        attr_a_h = nc.dram_tensor("sorted_attr_32", (ROWS, EA), F32, kind="Internal").ap()
        attr_b_h = nc.dram_tensor("sorted_attr_17", (ROWS, EB), F32, kind="Internal").ap()
        tab_h = nc.dram_tensor("node_rows", (NP, D), F32, kind="Internal").ap()
        tab2_h = nc.dram_tensor("node_rows_wide", (NP, 2 * D), F32, kind="Internal").ap()
        tab_v = tab_h.rearrange("(b p) d -> p b d", p=P)
        tab2_v = tab2_h.rearrange("(b p) d -> p b d", p=P)

        x = sbuf("x", [P, NB, D])
        h = sbuf("h", [P, NB, D])
        accT = sbuf("accT", [D + 1, NP])
        src_all = sbuf("src_all", [P, T], I32)
        lane_all = sbuf("lane_all", [P, T])
        tile_col = sbuf("tile_col", [1, T], I32)
        tile_row = sbuf("tile_row", [1, T], I32)
        tile_node = sbuf("tile_node", [P, T])
        disorder = sbuf("disorder", [1, 1], I32)
        rdeg = sbuf("rdeg", [P, NB])
        dinv = sbuf("dinv", [P, NB])
        iota = sbuf("iota", [P, P])
        ident = sbuf("ident", [P, P])
        s_sum = sbuf("s_sum", [P, NB])
        s_var = sbuf("s_var", [P, NB])
        s_std = sbuf("s_std", [P, NB])
        s_rstd = sbuf("s_rstd", [P, NB])

        w0 = sbuf("w0", [D + 1, D + 1])
        w1n = sbuf("w1n", [D, 2 * D])
        w1e = sbuf("w1e", [KA, 2 * D])
        w2m = sbuf("w2m", [D + 1, D])
        gw2 = sbuf("gw2", [P, D])
        gb2 = sbuf("gb2", [P, 1])
        half_gb2 = sbuf("half_gb2", [P, 1])
        u1x = sbuf("u1x", [D, D])
        u1a = sbuf("u1a", [D, D])
        ub1 = sbuf("ub1", [D, 1])
        u2 = sbuf("u2", [D + 1, D])
        lng = sbuf("lng", [P, D])
        lnb = sbuf("lnb", [P, D])
        w17 = sbuf("w17", [KB, D])
        w2w = sbuf("w2w", [D + 1, D])
        wsT = sbuf("wsT", [D + 1, D])
        bn_row = sbuf("bn_row", [D + 1, D])
        wnT = sbuf("wnT", [D, D])
        winT = sbuf("winT", [D + 1, D])
        gcnT = sbuf("gcnT", [D, 3, D])
        gcnb = sbuf("gcnb", [P, 3, D])
        woutT = sbuf("woutT", [D + 1, D])

        loaded = sem("loaded")
        made = sem("made")
        vec = sem("vec")
        act = sem("act")
        counted = sem("counted")
        offsets = sem("offsets")
        steps_up = sem("steps_up")
        columns = sem("columns")
        tails = sem("tails")
        rest = sem("rest")
        laid = sem("laid")
        paired = sem("paired")
        copied = sem("copied")
        centred = sem("centred")
        squared = sem("squared")
        variance = sem("variance")
        deviated = sem("deviated")
        normed = sem("normed")
        stored = sem("stored")
        turned = sem("turned")
        turned_kept = sem("turned_kept")
        product = sem("product")
        product_kept = sem("product_kept")
        hidden = sem("hidden")
        hidden_kept = sem("hidden_kept")
        node_done = sem("node_done")
        stage_in = [sem(f"stage_in{k}") for k in range(2)]
        placed = sem("placed")
        scattered = [[sem(f"scattered_{a}{k}") for a in ("pairs", "a", "b")] for k in range(2)]
        scatter_go = sem("scatter_go")
        idx_ready = [sem(f"idx_ready{k}") for k in range(GPI)]
        attr_ready = [sem(f"attr_ready{k}") for k in range(GPI)]
        gather_go = sem("gather_go")
        passed_t = sem("passed_t")
        passed_v = sem("passed_v")
        gathered = [sem(f"gathered{k}") for k in range(GPI)]
        src_kept = sem("src_kept")
        fields = sem("fields")
        hot = sem("hot")
        summed = sem("summed")
        added = sem("added")
        attrT = sem("attrT")
        attrT_kept = sem("attrT_kept")
        edge_mm = sem("edge_mm")
        edge_used = sem("edge_used")
        edge_act = sem("edge_act")
        edge_mm2 = sem("edge_mm2")
        logits = sem("logits")
        gate_ready = sem("gate_ready")
        gate1 = sem("gate1")

        def dyn(start, n):
            return bass.ds(start, n)

        sort_ctx = ExitStack()
        with sort_ctx:
            def tmp(name, shape, dt=F32):
                return sbuf(name, shape, dt, sort_ctx)
            dst_i = tmp("dst_i", [P, COLS], I32)
            src_i = tmp("src_i", [P, COLS], I32)
            pairs = tmp("pairs", [P, COLS, 2], I32)
            next_i = tmp("next_i", [P, 1], I32)
            next_f = tmp("next_f", [P, 1])
            bad = tmp("bad", [P, 1])
            blk_i = tmp("blk_i", [P, COLS], I32)
            blk_f = tmp("blk_f", [P, COLS])
            mask = tmp("mask", [P, COLS])
            ones_c = tmp("ones_c", [P, COLS])
            rank = tmp("rank", [P, COLS])
            pos = tmp("pos", [P, COLS])
            count = tmp("count", [P, NB])
            before = tmp("before", [P, P])
            ones_p = tmp("ones_p", [P, P])
            offs = tmp("offs", [P, NB])
            e_end = tmp("e_end", [P, NB])
            e_start = tmp("e_start", [P, NB])
            tiles_i = tmp("tiles_i", [P, NB], I32)
            tiles_f = tmp("tiles_f", [P, NB])
            total = tmp("total", [P, NB])
            t_end = tmp("t_end", [P, NB])
            t_start = tmp("t_start", [P, NB])
            gap = tmp("gap", [NB, NB])
            gap_step = tmp("gap_step", [NB, NB])
            start_col = tmp("start_col", [NB, 1])
            gap_col = tmp("gap_col", [NB, 1])
            diag = tmp("diag", [NB, NB])
            diag2 = tmp("diag2", [NB, NB])
            tile_no = tmp("tile_no", [NB, T])
            row_f = tmp("row_f", [1, T])
            block_w = tmp("block_w", [NB, P])
            HC = SC // 2
            st_a = tmp("st_a", [P, 2, HC, EA])
            st_b = tmp("st_b", [P, 2, HC, EB])
            pair_ring = tmp("pair_ring", [P, 2, HC, 2], I32)
            pos_ring = tmp("pos_ring", [P, 2, HC], I32)
            no_pair = tmp("no_pair", [P, 2], I32)
            ZR = 8
            zeros = tmp("zeros", [P, ZR * EA])
            assert (PADDED - E) % ZR == 0 and (PADDED - E) // ZR <= P
            PC = T // 4
            assert T % 4 == 0 and PC <= 512

            ps_ctx = sort_ctx.enter_context(nc.psum_tensor("ps_sort", [P, 8, 512], F32))
            ps = ps_ctx
            with nc.Block("sort") as block:
                @block.sync
                def _(sp):
                    sp.wait_ge(vec.sem, 3)
                    for t, a in ((dst_i, dst_in), (src_i, src_in)):
                        lanes = a[0:(P - 1) * COLS].rearrange("(p j) -> p j", j=COLS)
                        last = a[(P - 1) * COLS:E].rearrange("(p j) -> p j", p=1)
                        sp.dma_start(t[0:96, :], lanes[0:96, :]).then_inc(loaded.sem, 16)
                        sp.dma_start(t[96:P - 1, :], lanes[96:P - 1, :]).then_inc(loaded.sem, 16)
                        sp.dma_start(t[P - 1:P, 0:LAST], last).then_inc(loaded.sem, 16)
                        if t is dst_i:
                            sp.dma_start(next_i[0:P - 2, :], lanes[1:P - 1, 0:1], allow_slow_non_contiguous=True).then_inc(loaded.sem, 16)
                            sp.dma_start(next_i[P - 2:P - 1, :], last[:, 0:1]).then_inc(loaded.sem, 16)
                    sp.wait_ge(rest.sem, 2)
                    sp.dma_start(pairs_h[PADDED:ROWS, :], no_pair[:, :]).then_inc(tails.sem, 16)
                    sp.dma_start(attr_a_h[PADDED:ROWS, :], zeros[:, 0:EA]).then_inc(tails.sem, 16)
                    sp.dma_start(attr_b_h[PADDED:ROWS, :], zeros[:, 0:EB]).then_inc(tails.sem, 16)
                    sp.wait_ge(tails.sem, 48)

                @block.scalar
                def _(a):
                    a.wait_ge(vec.sem, 5)
                    loads = [
                        (x[:, 0:FULL, :], x_in[0:FULL * P, :].rearrange("(b p) d -> p b d", p=P)),
                        (x[0:REST, FULL, :], x_in[FULL * P:N, :]),
                        (w0[0:D, 0:D], w["L0_gnn_W"]), (w0[D:D + 1, 0:D], w["L0_gnn_b"]),
                        (w1n[:, 0:D], w["L1_gnn_mW1"][0:D, :]), (w1n[:, D:2 * D], w["L1_gnn_gW1"][0:D, :]),
                        (w1e[0:EA, 0:D], w["L1_gnn_mW1"][D:D + EA, :]),
                        (w1e[0:EA, D:2 * D], w["L1_gnn_gW1"][D:D + EA, :]),
                        (w1e[EA:KA, 0:D], w["L1_gnn_mb1"]), (w1e[EA:KA, D:2 * D], w["L1_gnn_gb1"]),
                        (w2m[0:D, :], w["L1_gnn_mW2"]), (w2m[D:D + 1, :], w["L1_gnn_mb2"]),
                        (gw2[:, :], w["L1_gnn_gW2"].to_broadcast([P, D])),
                        (gb2[:, :], w["L1_gnn_gb2"].to_broadcast([P, 1])),
                        (u1x[:, :], w["L1_gnn_uW1"][0:D, :]), (u1a[:, :], w["L1_gnn_uW1"][D:2 * D, :]),
                        (ub1[:, :], w["L1_gnn_ub1"]),
                        (u2[0:D, :], w["L1_gnn_uW2"]), (u2[D:D + 1, :], w["L1_gnn_ub2"]),
                        (lng[:, :], w["L1_gnn_ln_g"].to_broadcast([P, D])),
                        (lnb[:, :], w["L1_gnn_ln_b"].to_broadcast([P, D])),
                        (w17[0:EB, :], w["L2_gnn_W1"]), (w17[EB:KB, :], w["L2_gnn_b1"]),
                        (w2w[0:D, :], w["L2_gnn_W2"]), (w2w[D:D + 1, :], w["L2_gnn_b2"]),
                        (wsT[0:D, :], w["L2_gnn_Ws"]), (wsT[D:D + 1, :], w["L2_gnn_bs"]),
                        (bn_row[D:D + 1, :], w["L2_gnn_bn"]), (wnT[:, :], w["L2_gnn_Wn"]),
                        (winT[0:D, :], w["L3_gnn_W_in"]), (winT[D:D + 1, :], w["L3_gnn_b_in"]),
                        (gcnT[:, :, :], w["L3_gnn_gcn_W"]),
                        (gcnb[:, :, :], w["L3_gnn_gcn_b"].unsqueeze(0).to_broadcast([P, 3, D])),
                        (woutT[0:D, :], w["L3_gnn_W_out"]), (woutT[D:D + 1, :], w["L3_gnn_b_out"]),
                    ]
                    for dst, src in loads:
                        a.dma_start(dst, src).then_inc(stored.sem, 16)
                    a.wait_ge(stored.sem, 16 * len(loads))
                    stored.n = 16 * len(loads)

                @block.gpsimd
                def _(g):
                    g.iota(iota[:, :], [[1, P]], base=0, channel_multiplier=0,
                           allow_small_or_imprecise_dtypes=True).then_inc(made.sem, 1)
                    g.iota(tile_no[:, :], [[1, T]], base=0, channel_multiplier=0,
                           allow_small_or_imprecise_dtypes=True).then_inc(made.sem, 1)
                    g.iota(row_f[:, :], [[P, T]], base=0, channel_multiplier=0,
                           allow_small_or_imprecise_dtypes=True).then_inc(made.sem, 1)
                    g.memset(ident[:, :], 0.0).then_inc(made.sem, 1)
                    g.memset(ones_p[:, :], 1.0).then_inc(made.sem, 1)
                    g.memset(before[:, :], 1.0).then_inc(made.sem, 1)
                    g.wait_ge(made.sem, 6)
                    g.affine_select(out=ident[:, :], in_=ident[:, :], compare_op=ALU.not_equal, fill=1.0,
                                    base=0, pattern=[[-1, P]], channel_multiplier=1).then_inc(made.sem, 1)
                    g.affine_select(out=before[:, :], in_=before[:, :], compare_op=ALU.is_gt, fill=0.0,
                                    base=0, pattern=[[1, P]], channel_multiplier=-1).then_inc(made.sem, 1)
                    g.memset(block_w[:, :], float(P)).then_inc(made.sem, 1)
                MADE = 9

                @block.vector
                def _(v):
                    chain(v, vec, v.memset(dst_i[:, :], NP - 1))
                    chain(v, vec, v.memset(src_i[:, :], 0))
                    chain(v, vec, v.memset(next_i[:, :], NP - 1))
                    chain(v, vec, v.memset(x[:, FULL:NB, :], 0.0))
                    chain(v, vec, v.memset(w0[:, D:D + 1], 0.0))
                    chain(v, rest, v.memset(zeros[:, :], 0.0))
                    chain(v, vec, v.memset(no_pair[:, 0:1], 0))
                    v.memset(no_pair[:, 1:2], 2 * NP).then_inc(rest.sem, 1)
                    chain(v, vec, v.memset(w0[D:D + 1, D:D + 1], 1.0))
                    chain(v, vec, v.memset(ones_c[:, :], 1.0))
                    chain(v, vec, v.memset(st_a[:, :, :, :], 0.0))
                    chain(v, vec, v.memset(st_b[:, :, :, :], 0.0))
                    v.wait_ge(loaded.sem, 128)
                    chain(v, vec, v.tensor_scalar(blk_i[:, :], dst_i[:, :], 7, None, ALU.logical_shift_right))
                    chain(v, vec, v.tensor_copy(blk_f[:, :], blk_i[:, :]))
                    chain(v, vec, v.tensor_scalar(next_i[:, :], next_i[:, :], 7, None, ALU.logical_shift_right))
                    chain(v, vec, v.tensor_copy(next_f[:, :], next_i[:, :]))
                    chain(v, vec, v.tensor_copy(pairs[:, :, 0], src_i[:, :]))
                    chain(v, vec, v.tensor_copy(pairs[:, :, 1], dst_i[:, :]))
                    chain(v, vec, v.tensor_tensor(mask[:, 0:COLS - 1], blk_f[:, 0:COLS - 1], blk_f[:, 1:COLS],
                                                  ALU.is_gt))
                    chain(v, vec, v.tensor_tensor(mask[:, COLS - 1:COLS], blk_f[:, COLS - 1:COLS], next_f[:, :],
                                                  ALU.is_gt))
                    chain(v, vec, v.reduce_sum(bad[:, :], mask[:, :], AX.X))
                    v.wait_ge(made.sem, MADE)
                    n0 = vec.n
                    with v.Fori(0, NB) as b:
                        v.tensor_scalar(mask[:, :], blk_f[:, :], iota[:, dyn(b, 1)], None, ALU.is_equal,
                                        ALU.add, accum_out=count[:, dyn(b, 1)]).then_inc(vec.sem, 1)
                        v.wait_ge(vec.sem, n0 + b + 1)
                    vec.n = n0 + NB
                    v.wait_ge(vec.sem, vec.n)
                    chain(v, counted, v.tensor_copy(bad[:, :], bad[:, :]))
                    v.wait_ge(offsets.sem, 1)
                    chain(v, vec, v.tensor_scalar(disorder[:, :], ps[0:1, 6, 0:1], 1.0, None, ALU.min))
                    chain(v, vec, v.tensor_copy(total[:, :], ps[:, 1, 0:NB]))
                    chain(v, vec, v.tensor_scalar(tiles_f[:, :], total[:, :], float(P - 1), None, ALU.add))
                    chain(v, vec, v.tensor_copy(tiles_i[:, :], tiles_f[:, :]))
                    chain(v, vec, v.tensor_scalar(tiles_i[:, :], tiles_i[:, :], 7, None, ALU.logical_shift_right))
                    chain(v, vec, v.tensor_copy(tiles_f[:, :], tiles_i[:, :]))
                    for end, size, start in ((t_end, tiles_f, t_start), (e_end, total, e_start)):
                        chain(v, vec, v.tensor_tensor_scan(end[:, :], ones_c[:, 0:NB], size[:, :], 0.0,
                                                           ALU.mult, ALU.add))
                        chain(v, vec, v.tensor_tensor(start[:, :], end[:, :], size[:, :], ALU.subtract))
                    chain(v, vec, v.tensor_tensor(offs[:, :], e_start[:, :], ps[:, 0, 0:NB], ALU.add))
                    chain(v, vec, v.scalar_tensor_tensor(out=gap[:, :], in0=t_start[0:NB, :], scalar=float(P),
                                                         in1=e_start[0:NB, :], op0=ALU.mult, op1=ALU.subtract))
                    chain(v, vec, v.tensor_copy(gap_step[:, 0:1], gap[:, 0:1]))
                    chain(v, vec, v.tensor_tensor(gap_step[:, 1:NB], gap[:, 1:NB], gap[:, 0:NB - 1], ALU.subtract))
                    chain(v, vec, v.tensor_tensor(diag[:, :], ident[0:NB, 0:NB], t_start[0:NB, :], ALU.mult))
                    chain(v, vec, v.tensor_tensor(diag2[:, :], ident[0:NB, 0:NB], gap_step[:, :], ALU.mult))
                    chain(v, vec, v.reduce_sum(start_col[:, :], diag[:, :], AX.X))
                    chain(v, vec, v.reduce_sum(gap_col[:, :], diag2[:, :], AX.X))
                    chain(v, vec, v.tensor_scalar(tile_no[:, :], tile_no[:, :], start_col[:, 0:1], None,
                                                  ALU.is_ge))
                    v.tensor_copy(diag[:, :], diag[:, :]).then_inc(steps_up.sem, 1)
                    v.wait_ge(columns.sem, 1)
                    for c in range(4):
                        cs = slice(c * PC, (c + 1) * PC)
                        chain(v, vec, v.tensor_scalar(tile_node[:, cs], ps[:, 2 + c, 0:PC], -float(P), None, ALU.add))
                    chain(v, columns, v.tensor_copy(tile_col[:, :], tile_node[0:1, :]))
                    v.wait_ge(columns.sem, 3)
                    for c in range(4):
                        cs = slice(c * PC, (c + 1) * PC)
                        chain(v, vec, v.tensor_tensor(row_f[:, cs], row_f[:, cs], ps[0:1, 2 + c, 0:PC], ALU.subtract))
                    chain(v, vec, v.tensor_scalar(tile_row[:, :], row_f[:, :], float(PADDED), None, ALU.min))

                @block.tensor
                def _(pe):
                    pe.wait_ge(made.sem, MADE)
                    pe.wait_ge(counted.sem, 1)
                    pe.matmul(ps[:, 0, 0:NB], before[:, :], count[:, :], start=True, stop=True)
                    pe.matmul(ps[0:1, 6, 0:1], bad[:, :], ones_p[:, 0:1], start=True, stop=True)
                    pe.matmul(ps[:, 1, 0:NB], ones_p[:, :], count[:, :], start=True,
                              stop=True).then_inc(offsets.sem, 1)
                    pe.wait_ge(steps_up.sem, 1)
                    for c in range(4):
                        last = pe.matmul(ps[:, 2 + c, 0:PC], block_w[:, :], tile_no[:, c * PC:(c + 1) * PC],
                                         start=True, stop=True)
                    last.then_inc(columns.sem, 1)
                    pe.wait_ge(columns.sem, 2)
                    for c in range(4):
                        last = pe.matmul(ps[0:1, 2 + c, 0:PC], gap_col[:, :], tile_no[:, c * PC:(c + 1) * PC],
                                         start=True, stop=True)
                    last.then_inc(columns.sem, 1)

            with nc.Block("arrange") as block:
                a_rows = e32[0:(P - 1) * COLS, :].rearrange("(p j) c -> p j c", j=COLS)
                b_rows = e17[0:(P - 1) * COLS, :].rearrange("(p j) c -> p j c", j=COLS)
                LT = LAST // SC
                ST = COLS // SC
                ALL = ST * 16 * HC
                COPIES = 4

                def is_unsorted(eng):
                    return nc.values_load_multi_w_load_instructions(
                        disorder[0:1, 0:1], [eng], min_val=0, max_val=1,
                        skip_runtime_bounds_check_because="a count of at most one")[1][0] == 1

                def both(eng, body):
                    for k in range(2):
                        body(0, k)
                    with eng.Fori(1, ST) as i:
                        for k in range(2):
                            body(i, k)

                @block.sync
                def _(sp):
                    def load(i, k, last):
                        col = i * SC + k * HC
                        for a in (1, 2):
                            wait_past(sp, scattered[k][a].sem, 0, i * (16 * HC))
                        for st, rows, flat in ((st_a, a_rows, e32), (st_b, b_rows, e17)):
                            sp.dma_start(st[0:96, k], rows[0:96, dyn(col, HC), :]).then_inc(stage_in[k].sem, 16)
                            sp.dma_start(st[96:P - 1, k],
                                         rows[96:P - 1, dyn(col, HC), :]).then_inc(stage_in[k].sem, 16)
                            if last:
                                sp.dma_start(st[P - 1:P, k].rearrange("p j c -> p (j c)"),
                                             flat[dyn(col + (P - 1) * COLS, HC), :]
                                             .rearrange("(o j) c -> o (j c)", o=1)).then_inc(stage_in[k].sem, 16)
                            else:
                                sp.sem_inc(stage_in[k].sem, 16)
                    with sp.If(is_unsorted(SP)):
                        load(0, 0, True)
                        load(0, 1, True)
                        with sp.Fori(1, LT) as i:
                            load(i, 0, True)
                            load(i, 1, True)
                        with sp.Fori(LT, ST) as i:
                            load(i, 0, False)
                            load(i, 1, False)
                    with sp.Else():
                        sp.dma_start(pairs_h[0:PADDED, :].rearrange("(p j) c -> p (j c)", j=COLS),
                                     pairs[:, :, :].rearrange("p j c -> p (j c)")).then_inc(paired.sem, 16)
                        sp.wait_ge(paired.sem, 16)

                @block.scalar
                def _(a):
                    with a.If(is_unsorted(ACTE)):
                        a.sem_inc(copied.sem, 16 * COPIES)
                    with a.Else():
                        for to, of, c in ((attr_a_h, e32, EA), (attr_b_h, e17, EB)):
                            a.dma_start(to[0:E, :].rearrange("(p j) c -> p (j c)", p=1600),
                                        of.rearrange("(p j) c -> p (j c)", p=1600)).then_inc(copied.sem, 16)
                            a.dma_start(to[E:PADDED, :].rearrange("(p j) c -> p (j c)", j=ZR),
                                        zeros[0:(PADDED - E) // ZR, 0:ZR * c]).then_inc(copied.sem, 16)
                        a.wait_ge(copied.sem, 16 * COPIES)

                @block.vector
                def _(v):
                    with v.If(is_unsorted(DVE)):
                        n0 = n_if = vec.n
                        with v.Fori(0, NB) as b:
                            v.tensor_scalar(mask[:, :], blk_f[:, :], iota[:, dyn(b, 1)], None,
                                            ALU.is_equal).then_inc(vec.sem, 1)
                            v.wait_ge(vec.sem, n0 + b * 3 + 1)
                            v.tensor_tensor_scan(rank[:, :], ones_c[:, :], mask[:, :], offs[:, dyn(b, 1)],
                                                 ALU.mult, ALU.add).then_inc(vec.sem, 1)
                            v.wait_ge(vec.sem, n0 + b * 3 + 2)
                            v.sem_inc(passed_v.sem, 1)
                            v.copy_predicated(pos[:, :], mask[:, :].bitcast(I32), rank[:, :]).then_inc(vec.sem, 1)
                            v.wait_ge(vec.sem, n0 + b * 3 + 3)
                        vec.n = n0 + 3 * NB
                        v.wait_ge(vec.sem, vec.n)
                        chain(v, vec, v.tensor_scalar(pos[:, :], pos[:, :], -1.0, None, ALU.add))
                        chain(v, vec, v.tensor_copy(blk_i[:, :], pos[:, :]))

                        def body(i, k):
                            cols = dyn(i * SC + k * HC, HC)
                            for a in range(3):
                                wait_past(v, scattered[k][a].sem, 0, i * (16 * HC))
                            v.tensor_copy(pair_ring[:, k, :, :], pairs[:, cols, :])
                            v.tensor_copy(pos_ring[:, k, :], blk_i[:, cols]).then_inc(placed.sem, 1)
                        both(v, body)
                    with v.Else():
                        v.sem_inc(vec.sem, vec.n - n_if)

                @block.gpsimd
                def _(g):
                    with g.If(is_unsorted(POOL)):
                        def body(i, k):
                            g.wait_ge(placed.sem, i * 2 + k + 1)
                            g.wait_ge(stage_in[k].sem, (i + 1) * 96)
                            g.sem_inc(scatter_go.sem, 1)
                            for j in range(HC):
                                for a, (to, of) in enumerate(((pairs_h, pair_ring), (attr_a_h, st_a),
                                                              (attr_b_h, st_b))):
                                    g.indirect_dma_start(
                                        out=to, out_offset=bass.IndirectOffsetOnAxis(ap=pos_ring[:, k, j:j + 1], axis=0),
                                        in_=of[:, k, j, :], in_offset=None).then_inc(scattered[k][a].sem, 16)
                        both(g, body)
                        for k in range(2):
                            for a in range(3):
                                g.wait_ge(scattered[k][a].sem, ALL)
                    with g.Else():
                        g.sem_inc(scatter_go.sem, 1)

        hT = sbuf("hT", [D + 1, NP])
        wide = sbuf("wide", [P, GB, 2 * D])
        part = sbuf("part", [P, GB, D])
        part2 = sbuf("part2", [P, GB])
        aggT = sbuf("aggT", [D, GB * P])
        uT = sbuf("uT", [D + 1, GB * P])
        with nc.Block("ones") as block:
            @block.gpsimd
            def _(g):
                g.memset(hT[D:D + 1, :], 1.0).then_inc(made.sem, 1)
                g.memset(uT[D:D + 1, :], 1.0).then_inc(made.sem, 1)

            @block.vector
            def _(v):
                v.tensor_tensor(wsT[D:D + 1, :], wsT[D:D + 1, :], bn_row[D:D + 1, :], ALU.add).then_inc(vec.sem, 1)
                vec.n += 1
                v.tensor_scalar(half_gb2[:, :], gb2[:, :], 0.5, None, ALU.mult).then_inc(vec.sem, 1)
                vec.n += 1
                v.wait_ge(vec.sem, vec.n)

        def rows_bc(t):
            return t[:, :].unsqueeze(2).to_broadcast([P, NB, D])

        def norm_steps(block, src, dst, sq, finish, n_done=1):
            @block.vector
            def _(v):
                chain(v, vec, v.reduce_sum(s_sum[:, :], src[:, :, :], AX.X))
                chain(v, vec, v.tensor_scalar(s_sum[:, :], s_sum[:, :], 1.0 / D, None, ALU.mult))
                chain(v, centred, v.tensor_tensor(dst[:, :, :], src[:, :, :], rows_bc(s_sum), ALU.subtract))
                v.wait_ge(squared.sem, centred.n)
                chain(v, vec, v.reduce_sum(s_var[:, :], sq[:, :, :], AX.X))
                chain(v, variance, v.tensor_scalar(s_var[:, :], s_var[:, :], 1.0 / D, EPS, ALU.mult, ALU.add))
                v.wait_ge(deviated.sem, centred.n)
                chain(v, vec, v.reciprocal(s_rstd[:, :], s_std[:, :]))
                finish(v)

            @block.scalar
            def _(a):
                k = squared.n + 1
                a.wait_ge(centred.sem, k)
                a.activation(sq[:, :, :], dst[:, :, :], ACT.Square).then_inc(squared.sem, 1)
                a.wait_ge(variance.sem, k)
                a.activation(s_std[:, :], s_var[:, :], ACT.Sqrt).then_inc(deviated.sem, 1)
                squared.n = deviated.n = k

        def norm_relu(table):
            with nc.Block() as block, nc.sbuf_tensor(nc_name("sq"), [P, NB, D], F32) as sq:
                def finish(v):
                    chain(v, normed, v.scalar_tensor_tensor(out=h[:, :, :], in0=h[:, :, :], scalar=0.0,
                                                            in1=rows_bc(s_rstd), op0=ALU.max, op1=ALU.mult))
                norm_steps(block, x, h, sq, finish)

                @block.gpsimd
                def _(g):
                    g.memset(accT[:, :], 0.0).then_inc(made.sem, 1)
                if table:
                    @block.sync
                    def _(sp):
                        sp.wait_ge(normed.sem, normed.n)
                        sp.dma_start(tab_v, h[:, :, :]).then_inc(stored.sem, 16)
                        stored.n += 16
                        sp.wait_ge(stored.sem, stored.n)

        names = [0]

        def nc_name(s):
            names[0] += 1
            return f"{s}_{names[0]}"

        def transpose_nodes(src, dstT):
            with nc.psum_tensor(nc_name("psT"), [P, 2, 4, P], F32) as ps, nc.Block() as block:
                flat = ps[:, :, :, :].rearrange("p a b c -> p (a b c)")
                t0, k0 = turned.n, turned_kept.n

                @block.tensor
                def _(pe):
                    for s in range(GS):
                        pe.wait_ge(turned_kept.sem, s + k0)
                        for j in range(GB):
                            last = pe.transpose(ps[0:D, j // 4, j % 4, :],
                                                src[:, s * GB + j, :],
                                                ident[:, :])
                        last.then_inc(turned.sem, 1)

                @block.scalar
                def _(a):
                    with a.Fori(0, GS) as s:
                        a.wait_ge(turned.sem, s + (t0 + 1))
                        a.activation(dstT[0:D, dyn(s * (GB * P), GB * P)], flat[0:D, 0:GB * P],
                                     ACT.Copy).then_inc(turned_kept.sem, 1)
                turned.n += GS
                turned_kept.n += GS

        def node_product(terms, width, reader, use_scalar=False, extra=None):
            per = 1 if width > P else 4
            banks = -(-GB // (2 if width > P else 4))
            pitch = 512 // (2 if width > P else 4)
            with nc.psum_tensor(nc_name("psN"), [P, banks * 512 // pitch, pitch], F32) as ps, \
                    nc.Block() as block:
                p0, k0 = product.n, product_kept.n

                @block.tensor
                def _(pe):
                    for s in range(GS):
                        pe.wait_ge(product_kept.sem, s + k0)
                        for j in range(GB):
                            for n, (rowsT, k, wt) in enumerate(terms):
                                last = pe.matmul(ps[:, j, 0:width], rowsT[0:k, (s * GB + j) * P:(s * GB + j + 1) * P], wt,
                                                 start=(n == 0), stop=(n == len(terms) - 1))
                        last.then_inc(product.sem, 1)

                reader(block, ps, p0)
                if extra:
                    extra(block)
                product.n += GS
                product_kept.n += GS

        def edge_pass(kind, table, width, first=False):
            recs = kind != "copy"
            ctx = ExitStack()
            with ctx:
                def tmp(name, shape, dt=F32):
                    return sbuf(nc_name(name), shape, dt, ctx)

                def psum(name, shape):
                    return ctx.enter_context(nc.psum_tensor(nc_name(name), shape, F32))
                gw = width + 1 if first else width
                M = D + 1 if (first or kind == "gated") else D
                rows = tmp("rows", [P, GPI, G, gw])
                hots = tmp("hots", [P, 2, G, P])
                ps_sum = psum("ps_sum", [P, 2, G, P])
                if recs:
                    KK, ones_at, attr_h = (KA, EA, attr_a_h) if kind == "gated" else (KB, EB, attr_b_h)
                    attr_ring = tmp("attr_ring", [P, GPI, G, KK])
                idx_ring = tmp("idx_ring", [P, GPI, G, 2 if first else 1], I32)
                if kind == "gated":
                    ps_t = psum("ps_t", [P, 2, 512])
                    ps_e = psum("ps_e", [P, 2, 2, 512])
                    aT = tmp("aT", [KA, 2, 512])
                    act_ring = tmp("act_ring", [P, 3, G, 2, D + 1])
                    z = tmp("z", [P, 3, G])
                    th = tmp("th", [P, 3, G])
                    gate = tmp("gate", [P, 3, G])
                if kind == "filter":
                    ps_t = psum("ps_t", [P, 2, 512])
                    ps_e = psum("ps_e", [P, 2, 512])
                    ps_w = psum("ps_w", [P, 2, G, P])
                    aT = tmp("aT", [KB, 2, 512])
                    hid = tmp("hid", [D + 1, 2, 512])
                    msg = tmp("msg", [P, 3, G, D])

                base = {s: s.n for s in (idx_ready + attr_ready + gathered + [gather_go, fields, src_kept, hot, summed, added,
                                                                attrT, attrT_kept, edge_mm, edge_used, edge_act,
                                                                edge_mm2, logits, gate_ready, gate1])}
                rows_used = summed if kind == "copy" else edge_used
                block = ctx.enter_context(nc.Block())

                def past(eng, sig, q):
                    wait_past(eng, sig.sem, base[sig], q)

                @block.sync
                def _(sp):
                    def rows_of(q):
                        return nc.values_load_multi_w_load_instructions(
                            tile_row[0:1, dyn(q * G, G)], [SP], min_val=0, max_val=PADDED,
                            skip_runtime_bounds_check_because="clamped to the last tile's row")[1]

                    def load(q, turn, r):
                        past(sp, rows_used, q - (GPI - 1))
                        if first:
                            past(sp, src_kept, q - (GPI - 1))
                            for j, row in enumerate(rows_of(q)):
                                sp.dma_start(idx_ring[:, r, j, :], pairs_h[dyn(row, P), :])\
                                    .then_inc(idx_ready[r].sem, 16)
                        else:
                            sp.dma_start(idx_ring[:, r, :, 0], src_all[:, dyn(q * G, G)])\
                                .then_inc(idx_ready[r].sem, 16)
                        if recs:
                            for j, row in enumerate(rows_of(q)):
                                sp.dma_start(attr_ring[:, r, j, 0:ones_at], attr_h[dyn(row, P), :])\
                                    .then_inc(attr_ready[r].sem, 16)
                    turns(sp, [(load, 0)])

                @block.gpsimd
                def _(g):
                    if first:
                        g.memset(rows[:, :, :, D:D + 1], 1.0).then_inc(made.sem, 1)
                    if recs:
                        g.memset(attr_ring[:, :, :, ones_at:KK], 1.0).then_inc(made.sem, 1)
                    if kind == "gated":
                        g.memset(act_ring[:, :, :, 0, D:D + 1], 1.0).then_inc(made.sem, 1)
                    if kind == "filter":
                        g.wait_ge(made.sem, made.n + 1)
                        g.memset(hid[D:D + 1, :, :], 1.0).then_inc(made.sem, 1)

                    def gather(q, turn, r):
                        g.wait_ge(idx_ready[r].sem, base[idx_ready[r]] + (turn + 1) * (16 * (G if first else 1)))
                        g.sem_inc(gather_go.sem, 1)
                        for j in range(G):
                            idx = idx_ring[:, r, j, 0:1]
                            g.indirect_dma_start(
                                out=rows[:, r, j, 0:width], out_offset=None, in_=table,
                                in_offset=bass.IndirectOffsetOnAxis(ap=idx, axis=0)).then_inc(gathered[r].sem, 16)
                    turns(g, [(gather, 0)])
                made.n += first + 2 * recs

                def rows_in(eng, turn, r):
                    eng.wait_ge(gathered[r].sem, base[gathered[r]] + (turn + 1) * (16 * G))

                def hots_and_adds(v, with_hots, with_adds):
                    if with_adds:
                        qa, _, ra = with_adds
                        cols = nc.values_load_multi_w_load_instructions(
                            tile_col[0:1, dyn(qa * G, G)], [DVE], min_val=0, max_val=(NB - 1) * P,
                            skip_runtime_bounds_check_because="columns of the blocks, at most the last block's")[1]
                        past(v, summed, qa + 1)
                    if with_hots:
                        q, turn, r = with_hots
                        if first:
                            v.wait_ge(idx_ready[r].sem, base[idx_ready[r]] + (turn + 1) * (16 * G))
                            cs = dyn(q * G, G)
                            v.tensor_tensor(lane_all[:, cs], idx_ring[:, r, :, 1], tile_node[:, cs],
                                            ALU.subtract).then_inc(fields.sem, 1)
                            past(v, fields, q + 1)
                        if kind == "gated":
                            past(v, gate_ready, q + 1)
                            v.tensor_scalar(gate[:, r % 3, :], th[:, r % 3, :], 1.0, None,
                                            ALU.add).then_inc(gate1.sem, 1)
                            past(v, gate1, q + 1)
                        past(v, summed, q - 1)
                    for j in range(G):
                        if with_hots:
                            lane = lane_all[:, dyn(q * G + j, 1)]
                            if kind == "gated":
                                last = v.tensor_scalar(hots[:, r % 2, j, :], iota[:, :], lane,
                                                       gate[:, r % 3, j:j + 1], ALU.is_equal, ALU.mult)
                            else:
                                last = v.tensor_scalar(hots[:, r % 2, j, :], iota[:, :], lane, None, ALU.is_equal)
                            if j == G - 1:
                                last.then_inc(hot.sem, 1)
                        if with_adds:
                            past(v, added, qa * G + j)
                            acc = accT[0:M, dyn(cols[j], P)]
                            v.tensor_tensor(acc, acc, ps_sum[0:M, ra % 2, j, :], ALU.add).then_inc(added.sem, 1)

                def sum_targets(pe, q, turn, r, what):
                    past(pe, hot, q + 1)
                    past(pe, added, (q - 1) * G)
                    for j in range(G):
                        last = pe.matmul(ps_sum[0:M, r % 2, j, :], what(r, j), hots[:, r % 2, j, :],
                                         start=True, stop=True)
                    last.then_inc(summed.sem, 1)

                def transposes(pe, q, turn, r, kk):
                    pe.wait_ge(attr_ready[r].sem, base[attr_ready[r]] + (turn + 1) * (16 * G))
                    past(pe, attrT_kept, q - 1)
                    pe.sem_inc(passed_t.sem, 1)
                    for j in range(G):
                        last = pe.transpose(ps_t[0:kk, r % 2, j * P:(j + 1) * P], attr_ring[:, r, j, :],
                                            ident[:, :])
                    last.then_inc(attrT.sem, 1)

                def keep_attrT(a, q, turn, r, kk, free):
                    past(a, attrT, q + 1)
                    past(a, free, q - 1)
                    a.activation(aT[:, r % 2, :], ps_t[0:kk, r % 2, :], ACT.Copy).then_inc(attrT_kept.sem, 1)

                if kind == "copy":
                    @block.tensor
                    def _(pe):
                        def work(q, turn, r):
                            rows_in(pe, turn, r)
                            sum_targets(pe, q, turn, r, lambda r, j: rows[:, r, j, 0:M])
                        if first:
                            pe.wait_ge(made.sem, made.n)
                        turns(pe, [(work, 0)])

                    @block.vector
                    def _(v):
                        turns(v, [(lambda new, old: hots_and_adds(v, new, old), 0, 1)])
                    if first:
                        @block.scalar
                        def _(a):
                            def keep(q, turn, r):
                                a.wait_ge(idx_ready[r].sem, base[idx_ready[r]] + (turn + 1) * (16 * G))
                                a.activation(src_all[:, dyn(q * G, G)], idx_ring[:, r, :, 0],
                                             ACT.Copy).then_inc(src_kept.sem, 1)
                            turns(a, [(keep, 0)])

                if kind == "gated":
                    @block.tensor
                    def _(pe):
                        pe.wait_ge(made.sem, made.n)

                        def edge_part(q, turn, r):
                            past(pe, attrT_kept, q + 1)
                            past(pe, edge_used, q - 1)
                            for j in range(G):
                                last = pe.matmul(ps_e[:, r % 2, j // 2, (j % 2) * 2 * D:(j % 2 + 1) * 2 * D],
                                                 aT[:, r % 2, j * P:(j + 1) * P], w1e[:, :], start=True, stop=True)
                            last.then_inc(edge_mm.sem, 1)
                        turns(pe, [(lambda q, t, r: transposes(pe, q, t, r, KA), 0), (edge_part, 1),
                                   (lambda q, t, r: sum_targets(pe, q, t, r,
                                                                lambda r, j: act_ring[:, r % 3, j, 0, :]), 4)])

                    @block.scalar
                    def _(a):
                        def gelu(q, turn, r):
                            past(a, edge_used, q + 1)
                            v4 = act_ring[:, r % 3, :, :, 0:D].rearrange("p j a d -> p (j a) d")
                            a.activation(v4, v4, ACT.Gelu).then_inc(edge_act.sem, 1)

                        def tanh(q, turn, r):
                            past(a, logits, q + 1)
                            past(a, gate1, q - 2)
                            a.activation(th[:, r % 3, :], z[:, r % 3, :], ACT.Tanh, bias=half_gb2[:, 0:1],
                                         scale=0.5).then_inc(gate_ready.sem, 1)
                        turns(a, [(lambda q, t, r: keep_attrT(a, q, t, r, KA, edge_mm), 0), (gelu, 2), (tanh, 3)])

                    @block.vector
                    def _(v):
                        def combine(q, turn, r):
                            rows_in(v, turn, r)
                            past(v, edge_mm, q + 1)
                            past(v, summed, q - 2)
                            for c in range(2):
                                last = v.tensor_tensor(
                                    act_ring[:, r % 3, 2 * c:2 * c + 2, :, 0:D].rearrange("p j a d -> p (j a) d"),
                                    ps_e[:, r % 2, c, 0:4 * D].rearrange("p (j d) -> p j d", d=D),
                                    rows[:, r, 2 * c:2 * c + 2, :].rearrange("p j (a d) -> p (j a) d", d=D), ALU.add)
                            last.then_inc(edge_used.sem, 1)

                        def dots(q, turn, r):
                            past(v, edge_act, q + 1)
                            for j in range(G):
                                last = v.tensor_tensor_reduce(out=act_ring[:, r % 3, j, 1, 0:D], in0=act_ring[:, r % 3, j, 1, 0:D],
                                                              in1=gw2[:, :], scale=1.0, scalar=0.0, op0=ALU.mult,
                                                              op1=ALU.add, accum_out=z[:, r % 3, j:j + 1])
                            last.then_inc(logits.sem, 1)

                        turns(v, [(lambda new, old: hots_and_adds(v, new, old), 4, 5), (combine, 2), (dots, 3)])

                if kind == "filter":
                    @block.tensor
                    def _(pe):
                        pe.wait_ge(made.sem, made.n)

                        def layer1(q, turn, r):
                            past(pe, attrT_kept, q + 1)
                            past(pe, edge_act, q - 1)
                            pe.matmul(ps_e[0:D, r % 2, :], w17[:, :], aT[:, r % 2, :], start=True,
                                      stop=True).then_inc(edge_mm.sem, 1)

                        def layer2(q, turn, r):
                            past(pe, edge_act, q + 1)
                            past(pe, edge_used, q - 1)
                            for j in range(G):
                                last = pe.matmul(ps_w[:, r % 2, j, 0:D], hid[:, r % 2, j * P:(j + 1) * P], w2w[:, :],
                                                 start=True, stop=True)
                            last.then_inc(edge_mm2.sem, 1)
                        turns(pe, [(lambda q, t, r: transposes(pe, q, t, r, KB), 0), (layer1, 1), (layer2, 2),
                                   (lambda q, t, r: sum_targets(pe, q, t, r, lambda r, j: msg[:, r % 3, j, :]), 4)])

                    @block.scalar
                    def _(a):
                        def relu(q, turn, r):
                            past(a, edge_mm, q + 1)
                            past(a, edge_mm2, q - 1)
                            a.activation(hid[0:D, r % 2, :], ps_e[0:D, r % 2, :], ACT.Relu).then_inc(edge_act.sem, 1)
                        turns(a, [(lambda q, t, r: keep_attrT(a, q, t, r, KB, edge_mm), 0), (relu, 1)])

                    @block.vector
                    def _(v):
                        def times(q, turn, r):
                            rows_in(v, turn, r)
                            past(v, edge_mm2, q + 1)
                            past(v, summed, q - 2)
                            v.tensor_tensor(msg[:, r % 3, :, :], ps_w[:, r % 2, :, 0:D], rows[:, r, :, :],
                                            ALU.mult).then_inc(edge_used.sem, 1)
                        turns(v, [(lambda new, old: hots_and_adds(v, new, old), 4, 5), (times, 3)])

                for r in range(GPI):
                    uses = len(range(r, Q, GPI))
                    idx_ready[r].n += 16 * uses * (G if first else 1)
                    attr_ready[r].n += 16 * uses * G * recs
                    gathered[r].n += 16 * uses * G
                for s in (gather_go, hot, summed):
                    s.n += Q
                added.n += T
                if first:
                    fields.n += Q
                    src_kept.n += Q
                if kind != "copy":
                    for s in (attrT, attrT_kept, edge_mm, edge_used, edge_act):
                        s.n += Q
                if kind == "filter":
                    edge_mm2.n += Q
                if kind == "gated":
                    for s in (logits, gate_ready, gate1):
                        s.n += Q

        made.n = 11
        blocks_of = lambda t, s: t[:, dyn(s * GB, GB), :]
        part_bc = lambda t, s: t[:, dyn(s * GB, GB)].unsqueeze(2).to_broadcast([P, GB, D])

        def vector_reader(steps, n_chain):
            def reader(block, ps, p0):
                @block.vector
                def _(v):
                    v0 = vec.n
                    with v.Fori(0, GS) as s:
                        v.wait_ge(product.sem, s + (p0 + 1))
                        k = [0]

                        def link(ins):
                            k[0] += 1
                            ins.then_inc(vec.sem, 1)
                            v.wait_ge(vec.sem, s * n_chain + (v0 + k[0]))
                        last = steps(v, s, ps, link)
                        assert k[0] == n_chain
                        last.then_inc(product_kept.sem, 1)
                    vec.n = v0 + n_chain * GS
            return reader

        def store(view, src):
            with nc.Block() as block:
                @block.sync
                def _(sp):
                    sp.dma_start(view, src).then_inc(stored.sem, 16)
                    stored.n += 16
                    sp.wait_ge(stored.sem, stored.n)

        norm_relu(True)
        made.n += 1
        edge_pass("copy", tab_h, D, first=True)

        def mean_update(v, s, ps, link):
            link(v.tensor_copy(part2[:, :], ps[:, 0:GB, D]))
            link(v.tensor_scalar(dinv[:, dyn(s * GB, GB)], part2[:, :], 1.0, None, ALU.add))
            link(v.tensor_scalar(part2[:, :], part2[:, :], 1.0, None, ALU.max))
            link(v.reciprocal(rdeg[:, dyn(s * GB, GB)], part2[:, :]))
            link(v.tensor_tensor(part[:, :, :], ps[:, 0:GB, 0:D], part_bc(rdeg, s), ALU.mult))
            return v.tensor_tensor(blocks_of(x, s), blocks_of(x, s), part[:, :, :], ALU.add)
        node_product([(accT, D + 1, w0[:, :])], D + 1, vector_reader(mean_update, 5))
        with nc.Block() as block:
            @block.scalar
            def _(a):
                a.activation(dinv[:, :], dinv[:, :], ACT.Sqrt).then_inc(act.sem, 1)

            @block.vector
            def _(v):
                v.wait_ge(act.sem, 1)
                v.reciprocal(dinv[:, :], dinv[:, :]).then_inc(vec.sem, 1)
                vec.n += 1
                v.wait_ge(vec.sem, vec.n)

        norm_relu(False)
        made.n += 1
        transpose_nodes(h, hT)

        def keep_wide(block, ps, p0):
            @block.scalar
            def _(a):
                s0 = stored.n
                with a.Fori(0, GS) as s:
                    a.wait_ge(product.sem, s + (p0 + 1))
                    a.wait_ge(stored.sem, s * 16 + s0)
                    a.activation(wide[:, :, :], ps[:, 0:GB, 0:2 * D], ACT.Copy).then_inc(product_kept.sem, 1)

            @block.sync
            def _(sp):
                k0, s0 = product_kept.n, stored.n
                with sp.Fori(0, GS) as s:
                    sp.wait_ge(product_kept.sem, s + (k0 + 1))
                    sp.dma_start(tab2_v[:, dyn(s * GB, GB), :], wide[:, :, :]).then_inc(stored.sem, 16)
                stored.n += 16 * GS
                sp.wait_ge(stored.sem, stored.n)
        node_product([(hT, D, w1n[:, :])], 2 * D, keep_wide)
        edge_pass("gated", tab2_h, 2 * D)

        with nc.psum_tensor("ps_agg", [P, 2, 512], F32) as ps_a, nc.psum_tensor("ps_hid", [P, 2, 512], F32) as ps_b, \
                nc.psum_tensor("ps_upd", [P, 8, P], F32) as ps_c, nc.Block() as block:
            cuts = ((0, 512), (512, GB * P))
            flat_a = ps_a[:, :, :].rearrange("p a b -> p (a b)")
            flat_b = ps_b[:, :, :].rearrange("p a b -> p (a b)")
            hidden_kept.n += 1
            t0, tk0, h0, hk0, p0, k0 = turned.n, turned_kept.n, hidden.n, hidden_kept.n, product.n, product_kept.n

            @block.tensor
            def _(pe):
                with pe.Fori(0, GS) as s:
                    col = s * (GB * P)
                    pe.wait_ge(turned_kept.sem, s + tk0)
                    for n, (lo, hi) in enumerate(cuts):
                        last = pe.matmul(ps_a[0:D, n, 0:hi - lo], w2m[:, :], accT[:, dyn(col + lo, hi - lo)],
                                         start=True, stop=True)
                    last.then_inc(turned.sem, 1)
                    pe.wait_ge(turned_kept.sem, s + (tk0 + 1))
                    pe.wait_ge(hidden_kept.sem, s + hk0)
                    for n, (lo, hi) in enumerate(cuts):
                        pe.matmul(ps_b[0:D, n, 0:hi - lo], u1x[:, :], hT[0:D, dyn(col + lo, hi - lo)],
                                  start=True, stop=False)
                        last = pe.matmul(ps_b[0:D, n, 0:hi - lo], u1a[:, :], aggT[:, lo:hi], start=False, stop=True)
                    last.then_inc(hidden.sem, 1)
                    pe.wait_ge(hidden_kept.sem, s + (hk0 + 1))
                    pe.wait_ge(product_kept.sem, s + k0)
                    for j in range(GB):
                        last = pe.matmul(ps_c[:, j, 0:D], uT[:, j * P:(j + 1) * P], u2[:, :], start=True, stop=True)
                    last.then_inc(product.sem, 1)

            @block.scalar
            def _(a):
                a.sem_inc(hidden_kept.sem, 1)
                with a.Fori(0, GS) as s:
                    a.wait_ge(turned.sem, s + (t0 + 1))
                    a.activation(aggT[:, :], flat_a[0:D, 0:GB * P], ACT.Copy, scale=0.5).then_inc(turned_kept.sem, 1)
                    a.wait_ge(hidden.sem, s + (h0 + 1))
                    a.activation(uT[0:D, :], flat_b[0:D, 0:GB * P], ACT.Gelu, bias=ub1[:, 0:1])\
                        .then_inc(hidden_kept.sem, 1)

            @block.vector
            def _(v):
                with v.Fori(0, GS) as s:
                    v.wait_ge(product.sem, s + (p0 + 1))
                    v.tensor_tensor(blocks_of(h, s), blocks_of(h, s), ps_c[:, 0:GB, 0:D], ALU.add)\
                        .then_inc(product_kept.sem, 1)
            for sig in (turned, turned_kept, hidden, hidden_kept, product, product_kept):
                sig.n += GS

        def over_d(t):
            return t[:, :].unsqueeze(1).to_broadcast([P, NB, D])
        with nc.Block() as block, nc.sbuf_tensor("sq_l1", [P, NB, D], F32) as sq:
            def finish(v):
                chain(v, vec, v.tensor_tensor(h[:, :, :], h[:, :, :], rows_bc(s_rstd), ALU.mult))
                chain(v, vec, v.tensor_tensor(h[:, :, :], h[:, :, :], over_d(lng), ALU.mult))
                chain(v, vec, v.tensor_tensor(h[:, :, :], h[:, :, :], over_d(lnb), ALU.add))
                chain(v, vec, v.tensor_tensor(x[:, :, :], x[:, :, :], h[:, :, :], ALU.add))
            norm_steps(block, h, h, sq, finish)

        norm_relu(True)
        made.n += 1
        transpose_nodes(h, hT)
        edge_pass("filter", tab_h, D)

        def relu_add(v, s, ps, link):
            return v.scalar_tensor_tensor(out=blocks_of(x, s), in0=ps[:, 0:GB, 0:D], scalar=0.0,
                                          in1=blocks_of(x, s), op0=ALU.max, op1=ALU.add)
        node_product([(hT, D + 1, wsT[:, :]), (accT, D, wnT[:, :])], D, vector_reader(relu_add, 0))

        norm_relu(False)
        made.n += 1
        transpose_nodes(h, hT)
        cur = h
        scaled = sbuf("scaled", [P, NB, D])

        def enter(v, s, ps, link):
            link(v.tensor_scalar(blocks_of(cur, s), ps[:, 0:GB, 0:D], 0.0, None, ALU.max))
            return v.tensor_tensor(blocks_of(scaled, s), blocks_of(cur, s), part_bc(dinv, s), ALU.mult)
        node_product([(hT, D + 1, winT[:, :])], D, vector_reader(enter, 1))
        for layer in range(3):
            store(tab_v, scaled[:, :, :])
            transpose_nodes(scaled, accT)
            edge_pass("copy", tab_h, D)

            def convolve(v, s, ps, link):
                link(v.tensor_tensor(part[:, :, :], ps[:, 0:GB, 0:D], part_bc(dinv, s), ALU.mult))
                link(v.tensor_tensor(part[:, :, :], part[:, :, :],
                                     gcnb[:, layer, :].unsqueeze(1).to_broadcast([P, GB, D]), ALU.add))
                link(v.scalar_tensor_tensor(out=blocks_of(cur, s), in0=part[:, :, :], scalar=0.0,
                                            in1=blocks_of(cur, s), op0=ALU.max, op1=ALU.add))
                return v.tensor_tensor(blocks_of(scaled, s), blocks_of(cur, s), part_bc(dinv, s), ALU.mult)
            node_product([(accT, D, gcnT[:, layer, :])], D, vector_reader(convolve, 3))
        transpose_nodes(cur, hT)

        def finish_x(v, s, ps, link):
            return v.tensor_tensor(blocks_of(x, s), ps[:, 0:GB, 0:D], blocks_of(x, s), ALU.add)
        node_product([(hT, D + 1, woutT[:, :])], D, vector_reader(finish_x, 0))
        with nc.Block() as block:
            @block.sync
            def _(sp):
                sp.dma_start(out_h[0:FULL * P, :].rearrange("(b p) d -> p b d", p=P), x[:, 0:FULL, :])\
                    .then_inc(stored.sem, 16)
                sp.dma_start(out_h[FULL * P:N, :], x[0:REST, FULL, :]).then_inc(stored.sem, 16)
                stored.n += 32
                sp.wait_ge(stored.sem, stored.n)


_TURNED = ("L2_gnn_W1", "L2_gnn_W2", "L2_gnn_Ws", "L2_gnn_Wn", "L3_gnn_W_in", "L3_gnn_W_out")
_COLUMN = ("L1_gnn_ub1",)


def kernel(**inputs):
    import numpy as _np
    import concourse.bacc as _bacc
    from concourse import mybir as _mybir
    from concourse.bass_utils import run_bass_kernel_spmd as _run

    nc = _bacc.Bacc("TRN2", target_bir_lowering=False, num_devices=1)
    arrays, aps = {}, {}
    for name, value in inputs.items():
        a = _np.asarray(value)
        if name in _TURNED:
            a = a.T
        elif name == "L3_gnn_gcn_W":
            a = a.transpose(2, 0, 1)
        elif name == "L1_gnn_gW2":
            a = a.reshape(1, D)
        elif name in _COLUMN:
            a = a.reshape(-1, 1)
        elif a.ndim == 1 and name not in ("src", "dst"):
            a = a.reshape(1, -1)
        a = _np.ascontiguousarray(a)
        arrays[f"in_{name}"] = a
        aps[name] = nc.dram_tensor(f"in_{name}", a.shape, _mybir.dt.from_np(a.dtype), kind="ExternalInput").ap()
    aps["out"] = nc.dram_tensor("out_x", (N, D), _mybir.dt.float32, kind="ExternalOutput").ap()
    graph_kernel(nc, aps["x"], aps["src"], aps["dst"], aps["edge_attr_17"], aps["edge_attr_32"], aps)
    r = _run(nc, [arrays], core_ids=[0])
    return r.results[0]["out_x"]
```

```python
import numpy as np
import concourse.bass as bass
from concourse import mybir
from contextlib import ExitStack

F32 = mybir.dt.float32
I32 = mybir.dt.int32
BF16 = mybir.dt.bfloat16
ALU = mybir.AluOpType
ACT = mybir.ActivationFunctionType
AX = mybir.AxisListType
SP, PE, DVE, POOL, ACTE = (mybir.EngineType.SP, mybir.EngineType.PE, mybir.EngineType.DVE,
                           mybir.EngineType.Pool, mybir.EngineType.Activation)

P = 128
N, D, E = 6250, 96, 200000
EA, EB = 32, 17
NB = -(-N // P)
NP = NB * P
FULL = N // P
REST = N - FULL * P

SC = 16
COLS = -(-(-(-E // P)) // SC) * SC
LAST = E - (P - 1) * COLS
PADDED = COLS * P
ROWS = PADDED + P
assert 0 < LAST <= COLS and LAST % SC == 0

G = 4
GPI = 6
TILES = (E + NB * (P - 1)) // P
Q = -(-TILES // G)
T = Q * G

PIECES = Q // GPI
CP = 96
PIECE = E // (PIECES * CP) * CP
LEFT = E - PIECES * PIECE
COPIES = 2 * PIECES + 4
assert 0 < LEFT and Q % GPI > 0

KB = EB + 1
assert EA * G == P
ZR = 8

GB = 7
GS = NB // GB
EPS = 1e-5


class Signal:

    def __init__(self, ctx, nc, name):
        self.sem = ctx.enter_context(nc.semaphore(name))
        self.n = 0


def chain(eng, sig, ins):
    ins.then_inc(sig.sem, 1)
    sig.n += 1
    eng.wait_ge(sig.sem, sig.n)


def turns(eng, stages):
    def place(i, s, lag):
        q = i * GPI + (s - lag)
        if isinstance(i, int) and not 0 <= q < Q:
            return None
        return q, i if s >= lag else i - 1, (s - lag) % GPI

    def turn(i):
        for s in range(GPI):
            for work, *lags in stages:
                places = [place(i, s, lag) for lag in lags]
                if len(places) > 1 and any(places):
                    work(*places)
                elif places[0]:
                    work(*places[0])
    turn(0)
    with eng.Fori(1, Q // GPI) as i:
        turn(i)
    turn(Q // GPI)
    turn(Q // GPI + 1)


def wait_past(eng, sem, base, q):
    if isinstance(q, int) and q <= 0:
        return
    eng.wait_ge(sem, base + q)


def graph_kernel(nc, x_in, src_in, dst_in, e17, e32, w):
    out_h = w["out"]
    top = ExitStack()
    with top:
        def sem(name):
            return Signal(top, nc, name)

        def sbuf(name, shape, dt=F32, ctx=top):
            return ctx.enter_context(nc.sbuf_tensor(name, shape, dt))

        pairs_h = nc.dram_tensor("sorted_pairs", (ROWS, 2), I32, kind="Internal").ap()
        attr_a_h = nc.dram_tensor("sorted_attr_32", (ROWS, EA), F32, kind="Internal").ap()
        attr_b_h = nc.dram_tensor("sorted_attr_17", (ROWS, EB), F32, kind="Internal").ap()
        tab_h = nc.dram_tensor("node_rows", (NP, D), F32, kind="Internal").ap()
        tab2_h = nc.dram_tensor("node_rows_wide", (NP, 2 * D), F32, kind="Internal").ap()
        tab_v = tab_h.rearrange("(b p) d -> p b d", p=P)
        tab2_v = tab2_h.rearrange("(b p) d -> p b d", p=P)

        x = sbuf("x", [P, NB, D])
        h = sbuf("h", [P, NB, D])
        accT = sbuf("accT", [D + 1, NP])
        src_all = sbuf("src_all", [P, T], I32)
        lane_all = sbuf("lane_all", [P, T])
        tile_col = sbuf("tile_col", [1, T], I32)
        tile_row = sbuf("tile_row", [1, T], I32)
        tile_node = sbuf("tile_node", [P, T])
        disorder = sbuf("disorder", [1, 1], I32)
        rdeg = sbuf("rdeg", [P, NB])
        dinv = sbuf("dinv", [P, NB])
        iota = sbuf("iota", [P, P])
        ident = sbuf("ident", [P, P])
        s_sum = sbuf("s_sum", [P, NB])
        s_var = sbuf("s_var", [P, NB])
        s_std = sbuf("s_std", [P, NB])
        s_rstd = sbuf("s_rstd", [P, NB])

        w0 = sbuf("w0", [D + 1, D + 1])
        w1n = sbuf("w1n", [D + 1, 2 * D])
        w1e = sbuf("w1e", [P, G, 2 * D])
        zeros = sbuf("zeros", [P, ZR * EA])
        w2m = sbuf("w2m", [D + 1, D])
        gw2 = sbuf("gw2", [P, D])
        gb2 = sbuf("gb2", [P, 1])
        half_gb2 = sbuf("half_gb2", [P, 1])
        u1x = sbuf("u1x", [D, D])
        u1a = sbuf("u1a", [D, D])
        ub1 = sbuf("ub1", [D, 1])
        u2 = sbuf("u2", [D + 1, D])
        lng = sbuf("lng", [P, D])
        lnb = sbuf("lnb", [P, D])
        w17 = sbuf("w17", [KB, D])
        w2w = sbuf("w2w", [D + 1, D])
        wsT = sbuf("wsT", [D + 1, D])
        bn_row = sbuf("bn_row", [D + 1, D])
        wnT = sbuf("wnT", [D, D])
        winT = sbuf("winT", [D + 1, D])
        gcnT = sbuf("gcnT", [D, 3, D])
        gcnb = sbuf("gcnb", [P, 3, D])
        woutT = sbuf("woutT", [D + 1, D])

        loaded = sem("loaded")
        made = sem("made")
        vec = sem("vec")
        act = sem("act")
        counted = sem("counted")
        offsets = sem("offsets")
        steps_up = sem("steps_up")
        columns = sem("columns")
        tails = sem("tails")
        rest = sem("rest")
        laid = sem("laid")
        paired = sem("paired")
        copied = sem("copied")
        centred = sem("centred")
        squared = sem("squared")
        variance = sem("variance")
        deviated = sem("deviated")
        normed = sem("normed")
        stored = sem("stored")
        turned = sem("turned")
        turned_kept = sem("turned_kept")
        product = sem("product")
        product_kept = sem("product_kept")
        hidden = sem("hidden")
        hidden_kept = sem("hidden_kept")
        stage_in = [sem(f"stage_in{k}") for k in range(2)]
        placed = sem("placed")
        scattered = [[sem(f"scattered_{a}{k}") for a in ("pairs", "a", "b")] for k in range(2)]
        scatter_go = sem("scatter_go")
        idx_ready = [sem(f"idx_ready{k}") for k in range(GPI)]
        attr_ready = [sem(f"attr_ready{k}") for k in range(GPI)]
        gather_go = sem("gather_go")
        passed_t = sem("passed_t")
        passed_v = sem("passed_v")
        gathered = [sem(f"gathered{k}") for k in range(GPI)]
        src_kept = sem("src_kept")
        fields = sem("fields")
        hot = sem("hot")
        summed = sem("summed")
        added = sem("added")
        attrT = sem("attrT")
        attrT_kept = sem("attrT_kept")
        edge_mm = sem("edge_mm")
        edge_used = sem("edge_used")
        edge_act = sem("edge_act")
        edge_mm2 = sem("edge_mm2")
        logits = sem("logits")
        gate_ready = sem("gate_ready")
        gate1 = sem("gate1")

        def dyn(start, n):
            return bass.ds(start, n)

        sort_ctx = ExitStack()
        with sort_ctx:
            def tmp(name, shape, dt=F32):
                return sbuf(name, shape, dt, sort_ctx)
            dst_i = tmp("dst_i", [P, COLS], I32)
            src_i = tmp("src_i", [P, COLS], I32)
            pairs = tmp("pairs", [P, COLS, 2], I32)
            next_i = tmp("next_i", [P, 1], I32)
            next_f = tmp("next_f", [P, 1])
            bad = tmp("bad", [P, 1])
            blk_i = tmp("blk_i", [P, COLS], I32)
            blk_f = tmp("blk_f", [P, COLS])
            blk_h = tmp("blk_h", [P, COLS], BF16)
            mask_h = tmp("mask_h", [P, 3, COLS], BF16)
            mask = tmp("mask", [P, COLS])
            ones_c = tmp("ones_c", [P, COLS])
            rank = tmp("rank", [P, COLS])
            pos = tmp("pos", [P, COLS])
            count = tmp("count", [P, NB])
            before = tmp("before", [P, P])
            ones_p = tmp("ones_p", [P, P])
            offs = tmp("offs", [P, NB])
            e_end = tmp("e_end", [P, NB])
            e_start = tmp("e_start", [P, NB])
            tiles_i = tmp("tiles_i", [P, NB], I32)
            tiles_f = tmp("tiles_f", [P, NB])
            total = tmp("total", [P, NB])
            t_end = tmp("t_end", [P, NB])
            t_start = tmp("t_start", [P, NB])
            gap = tmp("gap", [NB, NB])
            gap_step = tmp("gap_step", [NB, NB])
            start_col = tmp("start_col", [NB, 1])
            gap_col = tmp("gap_col", [NB, 1])
            diag = tmp("diag", [NB, NB])
            diag2 = tmp("diag2", [NB, NB])
            tile_no = tmp("tile_no", [NB, T])
            row_f = tmp("row_f", [1, T])
            block_w = tmp("block_w", [NB, P])
            HC = SC // 2
            st_a = tmp("st_a", [P, 2, HC, EA])
            st_b = tmp("st_b", [P, 2, HC, EB])
            pair_ring = tmp("pair_ring", [P, 2, HC, 2], I32)
            pos_ring = tmp("pos_ring", [P, 2, HC], I32)
            no_pair = tmp("no_pair", [P, 2], I32)
            assert (PADDED - E) % ZR == 0 and (PADDED - E) // ZR <= P
            PC = T // 4
            assert T % 4 == 0 and PC <= 512

            ps_ctx = sort_ctx.enter_context(nc.psum_tensor("ps_sort", [P, 8, 512], F32))
            ps = ps_ctx
            with nc.Block("sort") as block:
                @block.sync
                def _(sp):
                    sp.wait_ge(vec.sem, 3)
                    for t, a in ((dst_i, dst_in), (src_i, src_in)):
                        lanes = a[0:(P - 1) * COLS].rearrange("(p j) -> p j", j=COLS)
                        last = a[(P - 1) * COLS:E].rearrange("(p j) -> p j", p=1)
                        sp.dma_start(t[0:96, :], lanes[0:96, :]).then_inc(loaded.sem, 16)
                        sp.dma_start(t[96:P - 1, :], lanes[96:P - 1, :]).then_inc(loaded.sem, 16)
                        sp.dma_start(t[P - 1:P, 0:LAST], last).then_inc(loaded.sem, 16)
                        if t is dst_i:
                            sp.dma_start(next_i[0:P - 2, :], lanes[1:P - 1, 0:1], allow_slow_non_contiguous=True).then_inc(loaded.sem, 16)
                            sp.dma_start(next_i[P - 2:P - 1, :], last[:, 0:1]).then_inc(loaded.sem, 16)
                    sp.wait_ge(rest.sem, 2)
                    sp.dma_start(pairs_h[PADDED:ROWS, :], no_pair[:, :]).then_inc(tails.sem, 16)
                    sp.dma_start(attr_a_h[PADDED:ROWS, :], zeros[:, 0:EA]).then_inc(tails.sem, 16)
                    sp.dma_start(attr_b_h[PADDED:ROWS, :], zeros[:, 0:EB]).then_inc(tails.sem, 16)
                    sp.wait_ge(tails.sem, 48)

                @block.scalar
                def _(a):
                    a.wait_ge(vec.sem, 6)
                    loads = [
                        (x[:, 0:FULL, :], x_in[0:FULL * P, :].rearrange("(b p) d -> p b d", p=P)),
                        (x[0:REST, FULL, :], x_in[FULL * P:N, :]),
                        (w0[0:D, 0:D], w["L0_gnn_W"]), (w0[D:D + 1, 0:D], w["L0_gnn_b"]),
                        (w1n[0:D, 0:D], w["L1_gnn_mW1"][0:D, :]), (w1n[0:D, D:2 * D], w["L1_gnn_gW1"][0:D, :]),
                        (w1n[D:D + 1, 0:D], w["L1_gnn_mb1"]), (w1n[D:D + 1, D:2 * D], w["L1_gnn_gb1"]),
                        (w2m[0:D, :], w["L1_gnn_mW2"]), (w2m[D:D + 1, :], w["L1_gnn_mb2"]),
                        (gw2[:, :], w["L1_gnn_gW2"].to_broadcast([P, D])),
                        (gb2[:, :], w["L1_gnn_gb2"].to_broadcast([P, 1])),
                        (u1x[:, :], w["L1_gnn_uW1"][0:D, :]), (u1a[:, :], w["L1_gnn_uW1"][D:2 * D, :]),
                        (ub1[:, :], w["L1_gnn_ub1"]),
                        (u2[0:D, :], w["L1_gnn_uW2"]), (u2[D:D + 1, :], w["L1_gnn_ub2"]),
                        (lng[:, :], w["L1_gnn_ln_g"].to_broadcast([P, D])),
                        (lnb[:, :], w["L1_gnn_ln_b"].to_broadcast([P, D])),
                        (w17[0:EB, :], w["L2_gnn_W1"]), (w17[EB:KB, :], w["L2_gnn_b1"]),
                        (w2w[0:D, :], w["L2_gnn_W2"]), (w2w[D:D + 1, :], w["L2_gnn_b2"]),
                        (wsT[0:D, :], w["L2_gnn_Ws"]), (wsT[D:D + 1, :], w["L2_gnn_bs"]),
                        (bn_row[D:D + 1, :], w["L2_gnn_bn"]), (wnT[:, :], w["L2_gnn_Wn"]),
                        (winT[0:D, :], w["L3_gnn_W_in"]), (winT[D:D + 1, :], w["L3_gnn_b_in"]),
                        (gcnT[:, :, :], w["L3_gnn_gcn_W"]),
                        (gcnb[:, :, :], w["L3_gnn_gcn_b"].unsqueeze(0).to_broadcast([P, 3, D])),
                        (woutT[0:D, :], w["L3_gnn_W_out"]), (woutT[D:D + 1, :], w["L3_gnn_b_out"]),
                    ]
                    for j in range(G):
                        quarter = w1e[j * EA:(j + 1) * EA, j, :]
                        loads.append((quarter[:, 0:D], w["L1_gnn_mW1"][D:D + EA, :]))
                        loads.append((quarter[:, D:2 * D], w["L1_gnn_gW1"][D:D + EA, :]))
                    for dst, src in loads:
                        a.dma_start(dst, src).then_inc(stored.sem, 16)
                    a.wait_ge(stored.sem, 16 * len(loads))
                    stored.n = 16 * len(loads)

                @block.gpsimd
                def _(g):
                    g.iota(iota[:, :], [[1, P]], base=0, channel_multiplier=0,
                           allow_small_or_imprecise_dtypes=True).then_inc(made.sem, 1)
                    g.iota(tile_no[:, :], [[1, T]], base=0, channel_multiplier=0,
                           allow_small_or_imprecise_dtypes=True).then_inc(made.sem, 1)
                    g.iota(row_f[:, :], [[P, T]], base=0, channel_multiplier=0,
                           allow_small_or_imprecise_dtypes=True).then_inc(made.sem, 1)
                    g.iota(pos[:, :], [[1, COLS]], base=1, channel_multiplier=COLS,
                           allow_small_or_imprecise_dtypes=True).then_inc(made.sem, 1)
                    g.memset(ident[:, :], 0.0).then_inc(made.sem, 1)
                    g.memset(ones_p[:, :], 1.0).then_inc(made.sem, 1)
                    g.memset(before[:, :], 1.0).then_inc(made.sem, 1)
                    g.wait_ge(made.sem, 7)
                    g.affine_select(out=ident[:, :], in_=ident[:, :], compare_op=ALU.not_equal, fill=1.0,
                                    base=0, pattern=[[-1, P]], channel_multiplier=1).then_inc(made.sem, 1)
                    g.affine_select(out=before[:, :], in_=before[:, :], compare_op=ALU.is_gt, fill=0.0,
                                    base=0, pattern=[[1, P]], channel_multiplier=-1).then_inc(made.sem, 1)
                    g.memset(block_w[:, :], float(P)).then_inc(made.sem, 1)
                MADE = 10

                @block.vector
                def _(v):
                    chain(v, vec, v.memset(dst_i[96:P, LAST:COLS], 2 * NP))
                    chain(v, vec, v.memset(src_i[96:P, LAST:COLS], 0))
                    chain(v, vec, v.memset(next_i[:, :], 2 * NP))
                    chain(v, vec, v.memset(x[:, FULL:NB, :], 0.0))
                    chain(v, vec, v.memset(w1e[:, :, :], 0.0))
                    chain(v, vec, v.memset(w0[:, D:D + 1], 0.0))
                    chain(v, rest, v.memset(zeros[:, :], 0.0))
                    chain(v, vec, v.memset(no_pair[:, 0:1], 0))
                    v.memset(no_pair[:, 1:2], 2 * NP).then_inc(rest.sem, 1)
                    chain(v, vec, v.memset(w0[D:D + 1, D:D + 1], 1.0))
                    chain(v, vec, v.memset(ones_c[:, :], 1.0))
                    chain(v, vec, v.memset(st_a[:, :, :, :], 0.0))
                    chain(v, vec, v.memset(st_b[:, :, :, :], 0.0))
                    v.wait_ge(loaded.sem, 128)
                    chain(v, vec, v.tensor_scalar(blk_i[:, :], dst_i[:, :], 7, None, ALU.logical_shift_right))
                    chain(v, vec, v.tensor_copy(blk_f[:, :], blk_i[:, :]))
                    chain(v, vec, v.tensor_copy(blk_h[:, :], blk_i[:, :]))
                    chain(v, vec, v.tensor_scalar(next_i[:, :], next_i[:, :], 7, None, ALU.logical_shift_right))
                    chain(v, vec, v.tensor_copy(next_f[:, :], next_i[:, :]))
                    chain(v, vec, v.tensor_copy(pairs[:, :, 0], src_i[:, :]))
                    chain(v, vec, v.tensor_copy(pairs[:, :, 1], dst_i[:, :]))
                    chain(v, vec, v.tensor_tensor(mask[:, 0:COLS - 1], blk_f[:, 0:COLS - 1], blk_f[:, 1:COLS],
                                                  ALU.is_gt))
                    chain(v, vec, v.tensor_tensor(mask[:, COLS - 1:COLS], blk_f[:, COLS - 1:COLS], next_f[:, :],
                                                  ALU.is_gt))
                    chain(v, vec, v.reduce_sum(bad[:, :], mask[:, :], AX.X))
                    v.wait_ge(made.sem, MADE)
                    n0 = vec.n
                    with v.Fori(0, GS) as i:
                        for k in range(GB):
                            b = i * GB + k
                            if k in (0, 3, 6):
                                v.wait_ge(vec.sem, b + n0)
                            v.tensor_scalar(mask_h[:, k % 3, :], blk_h[:, :], iota[:, dyn(b, 1)], None, ALU.is_equal,
                                            ALU.add, accum_out=count[:, dyn(b, 1)]).then_inc(vec.sem, 1)
                    vec.n = n0 + NB
                    v.wait_ge(vec.sem, vec.n)
                    chain(v, counted, v.tensor_copy(bad[:, :], bad[:, :]))
                    v.wait_ge(offsets.sem, 1)
                    chain(v, vec, v.tensor_scalar(disorder[:, :], ps[0:1, 6, 0:1], 1.0, None, ALU.min))
                    chain(v, vec, v.tensor_copy(total[:, :], ps[:, 1, 0:NB]))
                    chain(v, vec, v.tensor_scalar(tiles_f[:, :], total[:, :], float(P - 1), None, ALU.add))
                    chain(v, vec, v.tensor_copy(tiles_i[:, :], tiles_f[:, :]))
                    chain(v, vec, v.tensor_scalar(tiles_i[:, :], tiles_i[:, :], 7, None, ALU.logical_shift_right))
                    chain(v, vec, v.tensor_copy(tiles_f[:, :], tiles_i[:, :]))
                    for end, size, start in ((t_end, tiles_f, t_start), (e_end, total, e_start)):
                        chain(v, vec, v.tensor_tensor_scan(end[:, :], ones_c[:, 0:NB], size[:, :], 0.0,
                                                           ALU.mult, ALU.add))
                        chain(v, vec, v.tensor_tensor(start[:, :], end[:, :], size[:, :], ALU.subtract))
                    chain(v, vec, v.tensor_tensor(offs[:, :], e_start[:, :], ps[:, 0, 0:NB], ALU.add))
                    chain(v, vec, v.scalar_tensor_tensor(out=gap[:, :], in0=t_start[0:NB, :], scalar=float(P),
                                                         in1=e_start[0:NB, :], op0=ALU.mult, op1=ALU.subtract))
                    chain(v, vec, v.tensor_copy(gap_step[:, 0:1], gap[:, 0:1]))
                    chain(v, vec, v.tensor_tensor(gap_step[:, 1:NB], gap[:, 1:NB], gap[:, 0:NB - 1], ALU.subtract))
                    chain(v, vec, v.tensor_tensor(diag[:, :], ident[0:NB, 0:NB], t_start[0:NB, :], ALU.mult))
                    chain(v, vec, v.tensor_tensor(diag2[:, :], ident[0:NB, 0:NB], gap_step[:, :], ALU.mult))
                    chain(v, vec, v.reduce_sum(start_col[:, :], diag[:, :], AX.X))
                    chain(v, vec, v.reduce_sum(gap_col[:, :], diag2[:, :], AX.X))
                    chain(v, vec, v.tensor_scalar(tile_no[:, :], tile_no[:, :], start_col[:, 0:1], None,
                                                  ALU.is_ge))
                    v.tensor_copy(diag[:, :], diag[:, :]).then_inc(steps_up.sem, 1)
                    v.wait_ge(columns.sem, 1)
                    for c in range(4):
                        cs = slice(c * PC, (c + 1) * PC)
                        chain(v, vec, v.tensor_scalar(tile_node[:, cs], ps[:, 2 + c, 0:PC], -float(P), None, ALU.add))
                    chain(v, columns, v.tensor_copy(tile_col[:, :], tile_node[0:1, :]))
                    v.wait_ge(columns.sem, 3)
                    for c in range(4):
                        cs = slice(c * PC, (c + 1) * PC)
                        chain(v, vec, v.tensor_tensor(row_f[:, cs], row_f[:, cs], ps[0:1, 2 + c, 0:PC], ALU.subtract))
                    chain(v, vec, v.tensor_scalar(tile_row[:, :], row_f[:, :], float(PADDED), None, ALU.min))

                @block.tensor
                def _(pe):
                    pe.wait_ge(made.sem, MADE)
                    pe.wait_ge(counted.sem, 1)
                    pe.matmul(ps[:, 0, 0:NB], before[:, :], count[:, :], start=True, stop=True)
                    pe.matmul(ps[0:1, 6, 0:1], bad[:, :], ones_p[:, 0:1], start=True, stop=True)
                    pe.matmul(ps[:, 1, 0:NB], ones_p[:, :], count[:, :], start=True,
                              stop=True).then_inc(offsets.sem, 1)
                    pe.wait_ge(steps_up.sem, 1)
                    for c in range(4):
                        last = pe.matmul(ps[:, 2 + c, 0:PC], block_w[:, :], tile_no[:, c * PC:(c + 1) * PC],
                                         start=True, stop=True)
                    last.then_inc(columns.sem, 1)
                    pe.wait_ge(columns.sem, 2)
                    for c in range(4):
                        last = pe.matmul(ps[0:1, 2 + c, 0:PC], gap_col[:, :], tile_no[:, c * PC:(c + 1) * PC],
                                         start=True, stop=True)
                    last.then_inc(columns.sem, 1)

            def is_unsorted(eng):
                return nc.values_load_multi_w_load_instructions(
                    disorder[0:1, 0:1], [eng], min_val=0, max_val=1,
                    skip_runtime_bounds_check_because="a count of at most one")[1][0] == 1

            with nc.Block("arrange") as block:
                a_rows = e32[0:(P - 1) * COLS, :].rearrange("(p j) c -> p j c", j=COLS)
                b_rows = e17[0:(P - 1) * COLS, :].rearrange("(p j) c -> p j c", j=COLS)
                LT = LAST // SC
                ST = COLS // SC
                ALL = ST * 16 * HC
                def both(eng, body):
                    for k in range(2):
                        body(0, k)
                    with eng.Fori(1, ST) as i:
                        for k in range(2):
                            body(i, k)

                @block.sync
                def _(sp):
                    def load(i, k, last):
                        col = i * SC + k * HC
                        for a in (1, 2):
                            wait_past(sp, scattered[k][a].sem, 0, i * (16 * HC))
                        for st, rows, flat in ((st_a, a_rows, e32), (st_b, b_rows, e17)):
                            sp.dma_start(st[0:96, k], rows[0:96, dyn(col, HC), :]).then_inc(stage_in[k].sem, 16)
                            sp.dma_start(st[96:P - 1, k],
                                         rows[96:P - 1, dyn(col, HC), :]).then_inc(stage_in[k].sem, 16)
                            if last:
                                sp.dma_start(st[P - 1:P, k].rearrange("p j c -> p (j c)"),
                                             flat[dyn(col + (P - 1) * COLS, HC), :]
                                             .rearrange("(o j) c -> o (j c)", o=1)).then_inc(stage_in[k].sem, 16)
                            else:
                                sp.sem_inc(stage_in[k].sem, 16)
                    with sp.If(is_unsorted(SP)):
                        load(0, 0, True)
                        load(0, 1, True)
                        with sp.Fori(1, LT) as i:
                            load(i, 0, True)
                            load(i, 1, True)
                        with sp.Fori(LT, ST) as i:
                            load(i, 0, False)
                            load(i, 1, False)
                    with sp.Else():
                        sp.dma_start(pairs_h[0:PADDED, :].rearrange("(p j) c -> p (j c)", j=COLS),
                                     pairs[:, :, :].rearrange("p j c -> p (j c)")).then_inc(paired.sem, 16)
                        sp.wait_ge(paired.sem, 16)

                @block.vector
                def _(v):
                    with v.If(is_unsorted(DVE)):
                        n0 = n_if = vec.n
                        with v.Fori(0, NB) as b:
                            v.tensor_scalar(mask[:, :], blk_f[:, :], iota[:, dyn(b, 1)], None,
                                            ALU.is_equal).then_inc(vec.sem, 1)
                            v.wait_ge(vec.sem, n0 + b * 3 + 1)
                            v.tensor_tensor_scan(rank[:, :], ones_c[:, :], mask[:, :], offs[:, dyn(b, 1)],
                                                 ALU.mult, ALU.add).then_inc(vec.sem, 1)
                            v.wait_ge(vec.sem, n0 + b * 3 + 2)
                            v.sem_inc(passed_v.sem, 1)
                            v.copy_predicated(pos[:, :], mask[:, :].bitcast(I32), rank[:, :]).then_inc(vec.sem, 1)
                            v.wait_ge(vec.sem, n0 + b * 3 + 3)
                        vec.n = n0 + 3 * NB
                        v.wait_ge(vec.sem, vec.n)
                        chain(v, vec, v.tensor_scalar(pos[:, :], pos[:, :], -1.0, None, ALU.add))
                        chain(v, vec, v.tensor_copy(blk_i[:, :], pos[:, :]))

                        def body(i, k):
                            cols = dyn(i * SC + k * HC, HC)
                            for a in range(3):
                                wait_past(v, scattered[k][a].sem, 0, i * (16 * HC))
                            v.tensor_copy(pair_ring[:, k, :, :], pairs[:, cols, :])
                            v.tensor_copy(pos_ring[:, k, :], blk_i[:, cols]).then_inc(placed.sem, 1)
                        both(v, body)
                    with v.Else():
                        v.sem_inc(vec.sem, vec.n - n_if)

                @block.gpsimd
                def _(g):
                    with g.If(is_unsorted(POOL)):
                        def body(i, k):
                            g.wait_ge(placed.sem, i * 2 + k + 1)
                            g.wait_ge(stage_in[k].sem, (i + 1) * 96)
                            g.sem_inc(scatter_go.sem, 1)
                            for j in range(HC):
                                for a, (to, of) in enumerate(((pairs_h, pair_ring), (attr_a_h, st_a),
                                                              (attr_b_h, st_b))):
                                    g.indirect_dma_start(
                                        out=to, out_offset=bass.IndirectOffsetOnAxis(ap=pos_ring[:, k, j:j + 1], axis=0),
                                        in_=of[:, k, j, :], in_offset=None).then_inc(scattered[k][a].sem, 16)
                        both(g, body)
                        for k in range(2):
                            for a in range(3):
                                g.wait_ge(scattered[k][a].sem, ALL)
                    with g.Else():
                        g.sem_inc(scatter_go.sem, 1)

        hT = sbuf("hT", [D + 1, NP])
        wide = sbuf("wide", [P, 2, GB, 2 * D])
        part = sbuf("part", [P, 2, GB, D])
        part2 = sbuf("part2", [P, GB])
        aggT = sbuf("aggT", [D, 2, GB * P])
        uT = sbuf("uT", [D + 1, 2, GB * P])
        def step_of(s):
            return slice(s * GB, (s + 1) * GB)

        def spread(t, s):
            return t[:, step_of(s)].unsqueeze(2).to_broadcast([P, GB, D])

        def norm_steps(block, src, dst, sq, finish):
            c0, q0 = centred.n, squared.n

            @block.vector
            def _(v):
                def sums(s):
                    b = step_of(s)
                    chain(v, vec, v.reduce_sum(s_sum[:, b], src[:, b, :], AX.X))
                    chain(v, vec, v.tensor_scalar(s_sum[:, b], s_sum[:, b], 1.0 / D, None, ALU.mult))
                    v.tensor_tensor(dst[:, b, :], src[:, b, :], spread(s_sum, s), ALU.subtract)\
                        .then_inc(centred.sem, 1)

                def variances(s):
                    v.wait_ge(squared.sem, q0 + s + 1)
                    v.reduce_sum(s_var[:, step_of(s)], sq[:, step_of(s), :], AX.X).then_inc(vec.sem, 1)
                    vec.n += 1
                for s in range(GS):
                    sums(s)
                    if s > 0:
                        variances(s - 1)
                variances(GS - 1)
                v.wait_ge(vec.sem, vec.n)
                chain(v, variance, v.tensor_scalar(s_var[:, :], s_var[:, :], 1.0 / D, EPS, ALU.mult, ALU.add))
                v.wait_ge(centred.sem, c0 + GS)
                v.wait_ge(deviated.sem, variance.n)
                chain(v, vec, v.reciprocal(s_rstd[:, :], s_std[:, :]))
                for s in range(GS):
                    finish(v, s)

            @block.scalar
            def _(a):
                for s in range(GS):
                    a.wait_ge(centred.sem, c0 + s + 1)
                    a.activation(sq[:, step_of(s), :], dst[:, step_of(s), :], ACT.Square).then_inc(squared.sem, 1)
                a.wait_ge(variance.sem, variance.n)
                a.activation(s_std[:, :], s_var[:, :], ACT.Sqrt).then_inc(deviated.sem, 1)
            centred.n += GS
            squared.n += GS
            deviated.n += 1

        names = [0]

        def nc_name(s):
            names[0] += 1
            return f"{s}_{names[0]}"

        def turn_step(pe, ps, src, s):
            for j in range(GB):
                last = pe.transpose(ps[0:D, s % 2, j // 4, j % 4, :], src[:, s * GB + j, :], ident[:, :])
            last.then_inc(turned.sem, 1)

        def keep_turned(a, ps, dstT, s):
            a.activation(dstT[0:D, s * GB * P:(s + 1) * GB * P],
                         ps[0:D, s % 2, :, :, :].rearrange("p a b c -> p (a b c)")[:, 0:GB * P],
                         ACT.Copy).then_inc(turned_kept.sem, 1)

        def norm_relu(table, turn, first=False):
            with nc.psum_tensor(nc_name("psT"), [P, 2, 2, 4, P], F32) as ps, nc.Block() as block, \
                    nc.sbuf_tensor(nc_name("sq"), [P, NB, D], F32) as sq:
                n0, t0, k0 = normed.n, turned.n, turned_kept.n

                def finish(v, s):
                    b = step_of(s)
                    v.scalar_tensor_tensor(out=h[:, b, :], in0=h[:, b, :], scalar=0.0, in1=spread(s_rstd, s),
                                           op0=ALU.max, op1=ALU.mult).then_inc(normed.sem, 1)
                    if s == GS - 1:
                        v.wait_ge(normed.sem, n0 + GS)
                norm_steps(block, x, h, sq, finish)
                normed.n += GS

                @block.gpsimd
                def _(g):
                    if first:
                        g.memset(hT[D:D + 1, :], 1.0).then_inc(made.sem, 1)
                        g.memset(uT[D:D + 1, :, :], 1.0).then_inc(made.sem, 1)
                        g.wait_ge(made.sem, MADE + 2)
                    g.memset(accT[:, :], 0.0).then_inc(made.sem, 1)
                if table:
                    @block.sync
                    def _(sp):
                        for s in range(GS):
                            sp.wait_ge(normed.sem, n0 + s + 1)
                            sp.dma_start(tab_v[:, step_of(s), :], h[:, step_of(s), :]).then_inc(stored.sem, 16)
                        stored.n += 16 * GS
                        sp.wait_ge(stored.sem, stored.n)
                if turn:
                    @block.tensor
                    def _(pe):
                        for s in range(GS):
                            pe.wait_ge(normed.sem, n0 + s + 1)
                            if s >= 2:
                                pe.wait_ge(turned_kept.sem, k0 + s - 1)
                            turn_step(pe, ps, h, s)

                    @block.scalar
                    def _(a):
                        for s in range(GS):
                            a.wait_ge(turned.sem, t0 + s + 1)
                            keep_turned(a, ps, hT, s)
                    turned.n += GS
                    turned_kept.n += GS

        def transpose_nodes(src, dstT):
            with nc.psum_tensor(nc_name("psT"), [P, 2, 2, 4, P], F32) as ps, nc.Block() as block:
                t0, k0 = turned.n, turned_kept.n

                @block.tensor
                def _(pe):
                    for s in range(GS):
                        if s >= 2:
                            pe.wait_ge(turned_kept.sem, k0 + s - 1)
                        turn_step(pe, ps, src, s)

                @block.scalar
                def _(a):
                    for s in range(GS):
                        a.wait_ge(turned.sem, t0 + s + 1)
                        keep_turned(a, ps, dstT, s)
                turned.n += GS
                turned_kept.n += GS

        def node_product(terms, width, reader, then=None):
            pitch = 256 if width > P else P
            banks = -(-GB * pitch // 512)
            with ExitStack() as ctx:
                ps = ctx.enter_context(nc.psum_tensor(nc_name("psN"), [P, 2, banks * 512 // pitch, pitch], F32))
                if then:
                    ps_t = ctx.enter_context(nc.psum_tensor(nc_name("psT"), [P, 2, 2, 4, P], F32))
                block = ctx.enter_context(nc.Block())
                p0, k0, t0, tk0 = product.n, product_kept.n, turned.n, turned_kept.n

                @block.tensor
                def _(pe):
                    def turn(s):
                        pe.wait_ge(product_kept.sem, k0 + s + 1)
                        if s >= 2:
                            pe.wait_ge(turned_kept.sem, tk0 + s - 1)
                        turn_step(pe, ps_t, then[0], s)
                    for s in range(GS):
                        if s >= 2:
                            pe.wait_ge(product_kept.sem, k0 + s - 1)
                        for j in range(GB):
                            for n, (rowsT, k, wt) in enumerate(terms):
                                last = pe.matmul(ps[:, s % 2, j, 0:width],
                                                 rowsT[0:k, (s * GB + j) * P:(s * GB + j + 1) * P], wt,
                                                 start=(n == 0), stop=(n == len(terms) - 1))
                        last.then_inc(product.sem, 1)
                        if then and s > 0:
                            turn(s - 1)
                    if then:
                        turn(GS - 1)

                reader(block, ps, p0)
                product.n += GS
                product_kept.n += GS
                if then:
                    @block.scalar
                    def _(a):
                        for s in range(GS):
                            a.wait_ge(turned.sem, t0 + s + 1)
                            keep_turned(a, ps_t, then[1], s)

                    @block.sync
                    def _(sp):
                        for s in range(GS):
                            sp.wait_ge(product_kept.sem, k0 + s + 1)
                            sp.dma_start(tab_v[:, step_of(s), :], then[0][:, step_of(s), :])\
                                .then_inc(stored.sem, 16)
                        stored.n += 16 * GS
                        sp.wait_ge(stored.sem, stored.n)
                    turned.n += GS
                    turned_kept.n += GS

        def edge_pass(kind, table, width, first=False):
            recs = kind != "copy"
            ctx = ExitStack()
            with ctx:
                def tmp(name, shape, dt=F32):
                    return sbuf(nc_name(name), shape, dt, ctx)

                def psum(name, shape):
                    return ctx.enter_context(nc.psum_tensor(nc_name(name), shape, F32))
                gw = width + 1 if first else width
                M = D + 1 if (first or kind == "gated") else D
                rows = tmp("rows", [P, GPI, G, gw])
                hots = tmp("hots", [P, 2, G, P])
                ps_sum = psum("ps_sum", [P, 2, G, P])
                if recs:
                    attr_ring = tmp("attr_ring", [P, GPI, G, EA if kind == "gated" else KB])
                idx_ring = tmp("idx_ring", [P, GPI, G, 2 if first else 1], I32)
                if kind == "gated":
                    ps_e = psum("ps_e", [P, 2, 2, 512])
                    aT = tmp("aT", [P, 2, P])
                    act_ring = tmp("act_ring", [P, 3, G, 2, D + 1])
                    z = tmp("z", [P, 3, G])
                    th = tmp("th", [P, 3, G])
                    gate = tmp("gate", [P, 3, G])
                if kind == "filter":
                    ps_t = psum("ps_t", [P, 2, 512])
                    ps_e = psum("ps_e", [P, 2, 512])
                    ps_w = psum("ps_w", [P, 2, G, P])
                    aT = tmp("aT", [KB, 2, 512])
                    hid = tmp("hid", [D + 1, 2, 512])
                    msg = tmp("msg", [P, 3, G, D])

                base = {s: s.n for s in (idx_ready + attr_ready + gathered + [gather_go, fields, src_kept, hot, summed, added,
                                                                attrT, attrT_kept, edge_mm, edge_used, edge_act,
                                                                edge_mm2, logits, gate_ready, gate1])}
                rows_used = summed if kind == "copy" else edge_used
                block = ctx.enter_context(nc.Block())

                def past(eng, sig, q):
                    wait_past(eng, sig.sem, base[sig], q)

                @block.sync
                def _(sp):
                    if recs:
                        sp.wait_ge(copied.sem, 16 * COPIES)

                    def rows_of(q):
                        return nc.values_load_multi_w_load_instructions(
                            tile_row[0:1, dyn(q * G, G)], [SP], min_val=0, max_val=PADDED,
                            skip_runtime_bounds_check_because="clamped to the last tile's row")[1]

                    def load(q, turn, r):
                        past(sp, rows_used, q - (GPI - 1))
                        if first:
                            past(sp, src_kept, q - (GPI - 1))
                            for j, row in enumerate(rows_of(q)):
                                sp.dma_start(idx_ring[:, r, j, :], pairs_h[dyn(row, P), :])\
                                    .then_inc(idx_ready[r].sem, 16)
                        else:
                            sp.dma_start(idx_ring[:, r, :, 0], src_all[:, dyn(q * G, G)])\
                                .then_inc(idx_ready[r].sem, 16)
                        if recs:
                            for j, row in enumerate(rows_of(q)):
                                if kind == "gated":
                                    to = attr_ring[j * EA:(j + 1) * EA, r, :, :]
                                    of = attr_a_h[dyn(row, P), :].rearrange("(c i) f -> i c f", i=EA)
                                else:
                                    to, of = attr_ring[:, r, j, 0:EB], attr_b_h[dyn(row, P), :]
                                sp.dma_start(to, of).then_inc(attr_ready[r].sem, 16)
                    turns(sp, [(load, 0)])

                @block.gpsimd
                def _(g):
                    if first:
                        g.memset(rows[:, :, :, D:D + 1], 1.0).then_inc(made.sem, 1)
                    if kind == "filter":
                        g.memset(attr_ring[:, :, :, EB:KB], 1.0).then_inc(made.sem, 1)
                    if kind == "gated":
                        g.memset(act_ring[:, :, :, 0, D:D + 1], 1.0).then_inc(made.sem, 1)
                    if kind == "filter":
                        g.wait_ge(made.sem, made.n + 1)
                        g.memset(hid[D:D + 1, :, :], 1.0).then_inc(made.sem, 1)

                    def gather(q, turn, r):
                        g.wait_ge(idx_ready[r].sem, base[idx_ready[r]] + (turn + 1) * (16 * (G if first else 1)))
                        g.sem_inc(gather_go.sem, 1)
                        for j in range(G):
                            idx = idx_ring[:, r, j, 0:1]
                            g.indirect_dma_start(
                                out=rows[:, r, j, 0:width], out_offset=None, in_=table,
                                in_offset=bass.IndirectOffsetOnAxis(ap=idx, axis=0)).then_inc(gathered[r].sem, 16)
                    turns(g, [(gather, 0)])
                made.n += {"copy": int(first), "gated": 1, "filter": 2}[kind]

                def rows_in(eng, turn, r):
                    eng.wait_ge(gathered[r].sem, base[gathered[r]] + (turn + 1) * (16 * G))

                def hots_and_adds(v, with_hots, with_adds):
                    if with_adds:
                        qa, _, ra = with_adds
                        cols = nc.values_load_multi_w_load_instructions(
                            tile_col[0:1, dyn(qa * G, G)], [DVE], min_val=0, max_val=(NB - 1) * P,
                            skip_runtime_bounds_check_because="columns of the blocks, at most the last block's")[1]
                        past(v, summed, qa + 1)
                    if with_hots:
                        q, turn, r = with_hots
                        if first:
                            v.wait_ge(idx_ready[r].sem, base[idx_ready[r]] + (turn + 1) * (16 * G))
                            cs = dyn(q * G, G)
                            v.tensor_tensor(lane_all[:, cs], idx_ring[:, r, :, 1], tile_node[:, cs],
                                            ALU.subtract).then_inc(fields.sem, 1)
                            past(v, fields, q + 1)
                        if kind == "gated":
                            past(v, gate1, q + 1)
                        past(v, summed, q - 1)
                    for j in range(G):
                        if with_hots:
                            lane = lane_all[:, dyn(q * G + j, 1)]
                            if kind == "gated":
                                last = v.tensor_scalar(hots[:, r % 2, j, :], iota[:, :], lane,
                                                       gate[:, r % 3, j:j + 1], ALU.is_equal, ALU.mult)
                            else:
                                last = v.tensor_scalar(hots[:, r % 2, j, :], iota[:, :], lane, None, ALU.is_equal)
                            if j == G - 1:
                                last.then_inc(hot.sem, 1)
                        if with_adds:
                            past(v, added, qa * G + j)
                            acc = accT[0:M, dyn(cols[j], P)]
                            v.tensor_tensor(acc, acc, ps_sum[0:M, ra % 2, j, :], ALU.add).then_inc(added.sem, 1)

                def sum_targets(pe, q, turn, r, what):
                    past(pe, hot, q + 1)
                    past(pe, added, (q - 1) * G)
                    for j in range(G):
                        last = pe.matmul(ps_sum[0:M, r % 2, j, :], what(r, j), hots[:, r % 2, j, :],
                                         start=True, stop=True)
                    last.then_inc(summed.sem, 1)

                def transposes(pe, q, turn, r, kk):
                    pe.wait_ge(attr_ready[r].sem, base[attr_ready[r]] + (turn + 1) * (16 * G))
                    past(pe, attrT_kept, q - 1)
                    pe.sem_inc(passed_t.sem, 1)
                    for j in range(G):
                        last = pe.transpose(ps_t[0:kk, r % 2, j * P:(j + 1) * P], attr_ring[:, r, j, :],
                                            ident[:, :])
                    last.then_inc(attrT.sem, 1)

                def keep_attrT(a, q, turn, r, kk, free):
                    past(a, attrT, q + 1)
                    past(a, free, q - 1)
                    a.activation(aT[:, r % 2, :], ps_t[0:kk, r % 2, :], ACT.Copy).then_inc(attrT_kept.sem, 1)

                if kind == "copy":
                    @block.tensor
                    def _(pe):
                        def work(q, turn, r):
                            rows_in(pe, turn, r)
                            sum_targets(pe, q, turn, r, lambda r, j: rows[:, r, j, 0:M])
                        if first:
                            pe.wait_ge(made.sem, made.n)
                        turns(pe, [(work, 0)])

                    @block.vector
                    def _(v):
                        turns(v, [(lambda new, old: hots_and_adds(v, new, old), 0, 1)])
                    if first:
                        @block.scalar
                        def _(a):
                            def keep(q, turn, r):
                                a.wait_ge(idx_ready[r].sem, base[idx_ready[r]] + (turn + 1) * (16 * G))
                                a.activation(src_all[:, dyn(q * G, G)], idx_ring[:, r, :, 0],
                                             ACT.Copy).then_inc(src_kept.sem, 1)

                            def copy_attrs(q, turn, r):
                                if r != 0:
                                    return
                                for to, of, c in ((attr_a_h, e32, EA), (attr_b_h, e17, EB)):
                                    if isinstance(turn, int) and turn == PIECES:
                                        a.dma_start(to[E - LEFT:E, :], of[E - LEFT:E, :]).then_inc(copied.sem, 16)
                                        a.dma_start(to[E:PADDED, :].rearrange("(p j) c -> p (j c)", j=ZR),
                                                    zeros[0:(PADDED - E) // ZR, 0:ZR * c]).then_inc(copied.sem, 16)
                                    else:
                                        piece = dyn(turn * PIECE, PIECE)
                                        a.dma_start(to[piece, :].rearrange("(p j) c -> p (j c)", p=CP),
                                                    of[piece, :].rearrange("(p j) c -> p (j c)", p=CP))\
                                            .then_inc(copied.sem, 16)
                            with a.If(is_unsorted(ACTE)):
                                a.sem_inc(copied.sem, 16 * COPIES)
                                turns(a, [(keep, 0)])
                            with a.Else():
                                turns(a, [(keep, 0), (copy_attrs, 0)])

                if kind == "gated":
                    @block.tensor
                    def _(pe):
                        pe.wait_ge(made.sem, made.n)

                        def edge_part(q, turn, r):
                            past(pe, attrT_kept, q + 1)
                            past(pe, edge_used, q - 1)
                            for c in range(2):
                                last = pe.matmul(ps_e[:, r % 2, c, 0:4 * D], aT[:, r % 2, :],
                                                 w1e[:, 2 * c:2 * c + 2, :].rearrange("p j d -> p (j d)"),
                                                 start=True, stop=True)
                            last.then_inc(edge_mm.sem, 1)
                        turns(pe, [(edge_part, 1),
                                   (lambda q, t, r: sum_targets(pe, q, t, r,
                                                                lambda r, j: act_ring[:, r % 3, j, 0, :]), 3)])

                    @block.scalar
                    def _(a):
                        def gelu(q, turn, r):
                            past(a, edge_used, q + 1)
                            v4 = act_ring[:, r % 3, :, :, 0:D].rearrange("p j a d -> p (j a) d")
                            a.activation(v4, v4, ACT.Gelu).then_inc(edge_act.sem, 1)

                        def tanh(q, turn, r):
                            past(a, logits, q + 1)
                            past(a, gate1, q - 2)
                            a.activation(th[:, r % 3, :], z[:, r % 3, :], ACT.Tanh, bias=half_gb2[:, 0:1],
                                         scale=0.5).then_inc(gate_ready.sem, 1)
                        turns(a, [(tanh, 3), (gelu, 2)])

                    @block.vector
                    def _(v):
                        def turn_attrs(q, turn, r):
                            v.wait_ge(attr_ready[r].sem, base[attr_ready[r]] + (turn + 1) * (16 * G))
                            past(v, edge_mm, q - 1)
                            v.sem_inc(passed_v.sem, 1)
                            v.transpose(aT[:, r % 2, :], attr_ring[:, r, :, :].rearrange("p c f -> p (c f)"))\
                                .then_inc(attrT_kept.sem, 1)

                        def combine(q, turn, r):
                            rows_in(v, turn, r)
                            past(v, edge_mm, q + 1)
                            past(v, summed, q - 2)
                            for c in range(2):
                                last = v.tensor_tensor(
                                    act_ring[:, r % 3, 2 * c:2 * c + 2, :, 0:D].rearrange("p j a d -> p (j a) d"),
                                    ps_e[:, r % 2, c, 0:4 * D].rearrange("p (j d) -> p j d", d=D),
                                    rows[:, r, 2 * c:2 * c + 2, :].rearrange("p j (a d) -> p (j a) d", d=D), ALU.add)
                            last.then_inc(edge_used.sem, 1)

                        def dots(q, turn, r):
                            past(v, edge_act, q + 1)
                            for j in range(G):
                                last = v.tensor_tensor_reduce(out=act_ring[:, r % 3, j, 1, 0:D], in0=act_ring[:, r % 3, j, 1, 0:D],
                                                              in1=gw2[:, :], scale=1.0, scalar=0.0, op0=ALU.mult,
                                                              op1=ALU.add, accum_out=z[:, r % 3, j:j + 1])
                            last.then_inc(logits.sem, 1)

                        def gates(q, turn, r):
                            past(v, gate_ready, q + 1)
                            v.tensor_scalar(gate[:, r % 3, :], th[:, r % 3, :], 1.0, None,
                                            ALU.add).then_inc(gate1.sem, 1)

                        turns(v, [(dots, 3), (combine, 2), (gates, 3), (turn_attrs, 0),
                                  (lambda new, old: hots_and_adds(v, new, old), 3, 4)])

                if kind == "filter":
                    @block.tensor
                    def _(pe):
                        pe.wait_ge(made.sem, made.n)

                        def layer1(q, turn, r):
                            past(pe, attrT_kept, q + 1)
                            past(pe, edge_act, q - 1)
                            pe.matmul(ps_e[0:D, r % 2, :], w17[:, :], aT[:, r % 2, :], start=True,
                                      stop=True).then_inc(edge_mm.sem, 1)

                        def layer2(q, turn, r):
                            past(pe, edge_act, q + 1)
                            past(pe, edge_used, q - 1)
                            for j in range(G):
                                last = pe.matmul(ps_w[:, r % 2, j, 0:D], hid[:, r % 2, j * P:(j + 1) * P], w2w[:, :],
                                                 start=True, stop=True)
                            last.then_inc(edge_mm2.sem, 1)
                        turns(pe, [(lambda q, t, r: transposes(pe, q, t, r, KB), 0), (layer1, 1), (layer2, 2),
                                   (lambda q, t, r: sum_targets(pe, q, t, r, lambda r, j: msg[:, r % 3, j, :]), 4)])

                    @block.scalar
                    def _(a):
                        def relu(q, turn, r):
                            past(a, edge_mm, q + 1)
                            past(a, edge_mm2, q - 1)
                            a.activation(hid[0:D, r % 2, :], ps_e[0:D, r % 2, :], ACT.Relu).then_inc(edge_act.sem, 1)
                        turns(a, [(lambda q, t, r: keep_attrT(a, q, t, r, KB, edge_mm), 0), (relu, 1)])

                    @block.vector
                    def _(v):
                        def times(q, turn, r):
                            rows_in(v, turn, r)
                            past(v, edge_mm2, q + 1)
                            past(v, summed, q - 2)
                            v.tensor_tensor(msg[:, r % 3, :, :], ps_w[:, r % 2, :, 0:D], rows[:, r, :, :],
                                            ALU.mult).then_inc(edge_used.sem, 1)
                        turns(v, [(lambda new, old: hots_and_adds(v, new, old), 4, 5), (times, 3)])

                for r in range(GPI):
                    uses = len(range(r, Q, GPI))
                    idx_ready[r].n += 16 * uses * (G if first else 1)
                    attr_ready[r].n += 16 * uses * G * recs
                    gathered[r].n += 16 * uses * G
                for s in (gather_go, hot, summed):
                    s.n += Q
                added.n += T
                if first:
                    fields.n += Q
                    src_kept.n += Q
                if kind != "copy":
                    for s in (attrT_kept, edge_mm, edge_used, edge_act):
                        s.n += Q
                if kind == "filter":
                    attrT.n += Q
                    edge_mm2.n += Q
                if kind == "gated":
                    for s in (logits, gate_ready, gate1):
                        s.n += Q

        made.n = MADE + 2

        def vector_reader(steps):
            def reader(block, ps, p0):
                @block.vector
                def _(v):
                    for s in range(GS):
                        v.wait_ge(product.sem, p0 + s + 1)
                        steps(v, s, ps[:, s % 2, 0:GB, :], lambda ins: chain(v, vec, ins))\
                            .then_inc(product_kept.sem, 1)
            return reader

        norm_relu(True, False, first=True)
        made.n += 1
        edge_pass("copy", tab_h, D, first=True)

        def mean_update(v, s, ps, link):
            b = step_of(s)
            link(v.tensor_copy(part2[:, :], ps[:, :, D]))
            link(v.tensor_scalar(dinv[:, b], part2[:, :], 1.0, None, ALU.add))
            link(v.tensor_scalar(part2[:, :], part2[:, :], 1.0, None, ALU.max))
            link(v.reciprocal(rdeg[:, b], part2[:, :]))
            link(v.tensor_tensor(part[:, s % 2, :, :], ps[:, :, 0:D], spread(rdeg, s), ALU.mult))
            return v.tensor_tensor(x[:, b, :], x[:, b, :], part[:, s % 2, :, :], ALU.add)
        node_product([(accT, D + 1, w0[:, :])], D + 1, vector_reader(mean_update))
        with nc.Block() as block:
            @block.scalar
            def _(a):
                a.activation(dinv[:, :], dinv[:, :], ACT.Sqrt).then_inc(act.sem, 1)

            @block.vector
            def _(v):
                chain(v, vec, v.tensor_tensor(wsT[D:D + 1, :], wsT[D:D + 1, :], bn_row[D:D + 1, :], ALU.add))
                chain(v, vec, v.tensor_scalar(half_gb2[:, :], gb2[:, :], 0.5, None, ALU.mult))
                v.wait_ge(act.sem, 1)
                v.reciprocal(dinv[:, :], dinv[:, :]).then_inc(vec.sem, 1)
                vec.n += 1
                v.wait_ge(vec.sem, vec.n)

        norm_relu(False, True)
        made.n += 1

        def keep_wide(block, ps, p0):
            s0, k0 = stored.n, product_kept.n

            @block.scalar
            def _(a):
                for s in range(GS):
                    a.wait_ge(product.sem, p0 + s + 1)
                    if s >= 2:
                        a.wait_ge(stored.sem, s0 + 16 * (s - 1))
                    a.activation(wide[:, s % 2, :, :], ps[:, s % 2, 0:GB, 0:2 * D],
                                 ACT.Copy).then_inc(product_kept.sem, 1)

            @block.sync
            def _(sp):
                for s in range(GS):
                    sp.wait_ge(product_kept.sem, k0 + s + 1)
                    if s > 0:
                        sp.wait_ge(stored.sem, s0 + 16 * s)
                    sp.dma_start(tab2_v[:, step_of(s), :], wide[:, s % 2, :, :]).then_inc(stored.sem, 16)
                stored.n += 16 * GS
                sp.wait_ge(stored.sem, stored.n)
        node_product([(hT, D + 1, w1n[:, :])], 2 * D, keep_wide)
        edge_pass("gated", tab2_h, 2 * D)

        with nc.psum_tensor("ps_agg", [P, 2, 512], F32) as ps_a, nc.psum_tensor("ps_hid", [P, 2, 512], F32) as ps_b, \
                nc.psum_tensor("ps_upd", [P, 2, 8, P], F32) as ps_c, nc.Block() as block:
            cuts = ((0, 512), (512, GB * P))
            flat_a = ps_a[:, :, :].rearrange("p a b -> p (a b)")
            flat_b = ps_b[:, :, :].rearrange("p a b -> p (a b)")
            t0, tk0, h0, hk0, p0, k0 = turned.n, turned_kept.n, hidden.n, hidden_kept.n, product.n, product_kept.n

            @block.tensor
            def _(pe):
                def aggregate(s):
                    pe.wait_ge(turned_kept.sem, tk0 + s)
                    for n, (lo, hi) in enumerate(cuts):
                        last = pe.matmul(ps_a[0:D, n, 0:hi - lo], w2m[:, :],
                                         accT[:, s * GB * P + lo:s * GB * P + hi], start=True, stop=True)
                    last.then_inc(turned.sem, 1)

                def hidden_layer(s):
                    pe.wait_ge(turned_kept.sem, tk0 + s + 1)
                    if s > 0:
                        pe.wait_ge(hidden_kept.sem, hk0 + s)
                    for n, (lo, hi) in enumerate(cuts):
                        pe.matmul(ps_b[0:D, n, 0:hi - lo], u1x[:, :], hT[0:D, s * GB * P + lo:s * GB * P + hi],
                                  start=True, stop=False)
                        last = pe.matmul(ps_b[0:D, n, 0:hi - lo], u1a[:, :], aggT[:, s % 2, lo:hi],
                                         start=False, stop=True)
                    last.then_inc(hidden.sem, 1)

                def update(s):
                    pe.wait_ge(hidden_kept.sem, hk0 + s + 1)
                    if s >= 2:
                        pe.wait_ge(product_kept.sem, k0 + s - 1)
                    for j in range(GB):
                        last = pe.matmul(ps_c[:, s % 2, j, 0:D], uT[:, s % 2, j * P:(j + 1) * P], u2[:, :],
                                         start=True, stop=True)
                    last.then_inc(product.sem, 1)
                for s in range(GS + 2):
                    if s < GS:
                        aggregate(s)
                    if 0 < s <= GS:
                        hidden_layer(s - 1)
                    if s >= 2:
                        update(s - 2)

            @block.scalar
            def _(a):
                def keep_hidden(s):
                    a.wait_ge(hidden.sem, h0 + s + 1)
                    if s >= 2:
                        a.wait_ge(product.sem, p0 + s - 1)
                    a.activation(uT[0:D, s % 2, :], flat_b[0:D, 0:GB * P], ACT.Gelu, bias=ub1[:, 0:1])\
                        .then_inc(hidden_kept.sem, 1)
                for s in range(GS):
                    a.wait_ge(turned.sem, t0 + s + 1)
                    if s >= 2:
                        a.wait_ge(hidden.sem, h0 + s - 1)
                    a.activation(aggT[:, s % 2, :], flat_a[0:D, 0:GB * P], ACT.Copy, scale=0.5)\
                        .then_inc(turned_kept.sem, 1)
                    if s > 0:
                        keep_hidden(s - 1)
                keep_hidden(GS - 1)

            @block.vector
            def _(v):
                for s in range(GS):
                    v.wait_ge(product.sem, p0 + s + 1)
                    hs = h[:, step_of(s), :]
                    v.tensor_tensor(hs, hs, ps_c[:, s % 2, 0:GB, 0:D], ALU.add).then_inc(product_kept.sem, 1)
            for sig in (turned, turned_kept, hidden, hidden_kept, product, product_kept):
                sig.n += GS

        def over_d(t):
            return t[:, :].unsqueeze(1).to_broadcast([P, GB, D])
        with nc.Block() as block, nc.sbuf_tensor("sq_l1", [P, NB, D], F32) as sq:
            def finish(v, s):
                hs, xs = h[:, step_of(s), :], x[:, step_of(s), :]
                chain(v, vec, v.tensor_tensor(hs, hs, spread(s_rstd, s), ALU.mult))
                chain(v, vec, v.tensor_tensor(hs, hs, over_d(lng), ALU.mult))
                chain(v, vec, v.tensor_tensor(hs, hs, over_d(lnb), ALU.add))
                chain(v, vec, v.tensor_tensor(xs, xs, hs, ALU.add))
            norm_steps(block, h, h, sq, finish)

        norm_relu(True, True)
        made.n += 1
        edge_pass("filter", tab_h, D)

        def relu_add(v, s, ps, link):
            xs = x[:, step_of(s), :]
            return v.scalar_tensor_tensor(out=xs, in0=ps[:, :, 0:D], scalar=0.0, in1=xs, op0=ALU.max, op1=ALU.add)
        node_product([(hT, D + 1, wsT[:, :]), (accT, D, wnT[:, :])], D, vector_reader(relu_add))

        norm_relu(False, True)
        made.n += 1
        cur = h
        scaled = sbuf("scaled", [P, NB, D])

        def enter(v, s, ps, link):
            b = step_of(s)
            link(v.tensor_scalar(cur[:, b, :], ps[:, :, 0:D], 0.0, None, ALU.max))
            return v.tensor_tensor(scaled[:, b, :], cur[:, b, :], spread(dinv, s), ALU.mult)

        def convolve_of(layer, again):
            def convolve(v, s, ps, link):
                b = step_of(s)
                link(v.tensor_tensor(part[:, s % 2, :, :], ps[:, :, 0:D], spread(dinv, s), ALU.mult))
                link(v.tensor_tensor(part[:, s % 2, :, :], part[:, s % 2, :, :],
                                     gcnb[:, layer, :].unsqueeze(1).to_broadcast([P, GB, D]), ALU.add))
                last = v.scalar_tensor_tensor(out=cur[:, b, :], in0=part[:, s % 2, :, :], scalar=0.0,
                                              in1=cur[:, b, :], op0=ALU.max, op1=ALU.add)
                if not again:
                    return last
                link(last)
                return v.tensor_tensor(scaled[:, b, :], cur[:, b, :], spread(dinv, s), ALU.mult)
            return convolve
        node_product([(hT, D + 1, winT[:, :])], D, vector_reader(enter), then=(scaled, accT))
        for layer in range(3):
            edge_pass("copy", tab_h, D)
            again = layer < 2
            node_product([(accT, D, gcnT[:, layer, :])], D, vector_reader(convolve_of(layer, again)),
                         then=(scaled, accT) if again else None)
        transpose_nodes(cur, hT)

        def finish_x(v, s, ps, link):
            xs = x[:, step_of(s), :]
            return v.tensor_tensor(xs, ps[:, :, 0:D], xs, ALU.add)
        node_product([(hT, D + 1, woutT[:, :])], D, vector_reader(finish_x))
        with nc.Block() as block:
            @block.sync
            def _(sp):
                sp.dma_start(out_h[0:FULL * P, :].rearrange("(b p) d -> p b d", p=P), x[:, 0:FULL, :])\
                    .then_inc(stored.sem, 16)
                sp.dma_start(out_h[FULL * P:N, :], x[0:REST, FULL, :]).then_inc(stored.sem, 16)
                stored.n += 32
                sp.wait_ge(stored.sem, stored.n)


_TURNED = ("L2_gnn_W1", "L2_gnn_W2", "L2_gnn_Ws", "L2_gnn_Wn", "L3_gnn_W_in", "L3_gnn_W_out")
_COLUMN = ("L1_gnn_ub1",)


def kernel(**inputs):
    import numpy as _np
    import concourse.bacc as _bacc
    from concourse import mybir as _mybir
    from concourse.bass_utils import run_bass_kernel_spmd as _run

    nc = _bacc.Bacc("TRN2", target_bir_lowering=False, num_devices=1)
    arrays, aps = {}, {}
    for name, value in inputs.items():
        a = _np.asarray(value)
        if name in _TURNED:
            a = a.T
        elif name == "L3_gnn_gcn_W":
            a = a.transpose(2, 0, 1)
        elif name == "L1_gnn_gW2":
            a = a.reshape(1, D)
        elif name in _COLUMN:
            a = a.reshape(-1, 1)
        elif a.ndim == 1 and name not in ("src", "dst"):
            a = a.reshape(1, -1)
        a = _np.ascontiguousarray(a)
        arrays[f"in_{name}"] = a
        aps[name] = nc.dram_tensor(f"in_{name}", a.shape, _mybir.dt.from_np(a.dtype), kind="ExternalInput").ap()
    aps["out"] = nc.dram_tensor("out_x", (N, D), _mybir.dt.float32, kind="ExternalOutput").ap()
    graph_kernel(nc, aps["x"], aps["src"], aps["dst"], aps["edge_attr_17"], aps["edge_attr_32"], aps)
    r = _run(nc, [arrays], core_ids=[0])
    return r.results[0]["out_x"]
```
